# Optimizing a Trainium2 kernel written in Bass

```python
import numpy as np
import jax
import jax.numpy as jnp

def _softmax(x, axis=-1):
    return jax.nn.softmax(x, axis=axis)

def _gelu(x):
    return jax.nn.gelu(x, approximate=True)

def _silu(x):
    return jax.nn.silu(x)

def _sigmoid(x):
    return jax.nn.sigmoid(x)

def _layernorm(x, axis=-1, eps=1e-05):
    m = jnp.mean(x, axis=axis, keepdims=True)
    v = jnp.var(x, axis=axis, keepdims=True)
    return (x - m) / jnp.sqrt(v + eps)

def _scatter_add(tgt, idx, src, axis=0):
    return tgt.at[idx].add(src)

def _segment_sum(src, seg, n):
    return jax.ops.segment_sum(src, seg, n)
kernel_name = 'mk_hybrid_d1_jaxref_r8_1ef91c'

def setup_inputs(seed: int=0):
    np.random.seed(seed)
    _w = jnp.asarray

    def _L0_attn_a_setup():
        import jax, jax.numpy as jnp
        import numpy as np
        EPS = float(np.finfo(np.float32).eps)
        B, S, F_, E, H = (8, 512, 128, 128, 16)
        HD = E // H
        LAYER = 1
        LAMBDA_INIT = 0.8 - 0.6 * float(np.exp(-0.3 * (LAYER - 1)))
        SCALE = 1.0 / float(np.sqrt(E // 2))

        def _rms(x, g):
            return x * jax.lax.rsqrt(jnp.mean(x * x, axis=-1, keepdims=True) + EPS) * g
        key = jax.random.key(seed)
        ks = jax.random.split(key, 7)
        x = jax.random.normal(ks[0], (B, S, F_), jnp.float32)
        s = 0.02
        Wq = jax.random.normal(ks[1], (E, F_), jnp.float32) * s
        Wk = jax.random.normal(ks[2], (E, F_), jnp.float32) * s
        Wv = jax.random.normal(ks[3], (E, F_), jnp.float32) * s
        W1 = jax.random.normal(ks[4], (E, E), jnp.float32) * s
        W2 = jax.random.normal(ks[5], (E, E), jnp.float32) * s
        lambda_params = jnp.full((4,), 0.8, jnp.float32)
        g1 = jnp.ones((F_,), jnp.float32)
        g2 = jnp.ones((HD,), jnp.float32)
        g3 = jnp.ones((E,), jnp.float32)
        return dict(x=x, Wq=Wq, Wk=Wk, Wv=Wv, lambda_params=lambda_params, g1=g1, g2=g2, g3=g3, W1=W1, W2=W2)
    _L0_attn_a_in = _L0_attn_a_setup()

    def _L0_attn_b_setup():
        import jax, jax.numpy as jnp
        import numpy as np
        B, S, D_IN = (2, 256, 128)
        D_OUT, H, WINDOW = (128, 16, 64)
        HD = D_OUT // H
        key = jax.random.key(seed)
        k1, k2, k3, k4 = jax.random.split(key, 4)
        scale_in = 1.0 / np.sqrt(D_IN)
        scale_out = 1.0 / np.sqrt(D_OUT)
        return {'x': jax.random.normal(k1, (B, S, D_IN), dtype=jnp.float32), 'w_qkv': jax.random.normal(k2, (3 * D_OUT, D_IN), dtype=jnp.float32) * scale_in, 'w_out': jax.random.normal(k3, (D_OUT, D_OUT), dtype=jnp.float32) * scale_out, 'b_out': jax.random.normal(k4, (D_OUT,), dtype=jnp.float32) * scale_out}
    _L0_attn_b_in = _L0_attn_b_setup()

    def _L0_ffn_setup():
        import jax, jax.numpy as jnp
        import numpy as np
        TOP_K = 8
        NUM_EXPERTS = 32
        HIDDEN = 128
        EXPERT_DIM = 64
        key = jax.random.key(seed)
        k1, k2, k3, k4 = jax.random.split(key, 4)
        hidden_states = jax.random.normal(k1, (1, 256, HIDDEN), dtype=jnp.float32)
        gate_w = jax.random.normal(k2, (NUM_EXPERTS, HIDDEN), dtype=jnp.float32) * 0.02
        gate_up_w = jax.random.normal(k3, (NUM_EXPERTS, 2 * EXPERT_DIM, HIDDEN), dtype=jnp.float32) * 0.02
        down_w = jax.random.normal(k4, (NUM_EXPERTS, HIDDEN, EXPERT_DIM), dtype=jnp.float32) * 0.02
        return {'hidden_states': hidden_states, 'gate_w': gate_w, 'gate_up_w': gate_up_w, 'down_w': down_w}
    _L0_ffn_in = _L0_ffn_setup()
    _d = {'L0_attn_a_x': _L0_attn_a_in['x'], 'L0_attn_a_Wq': _L0_attn_a_in['Wq'], 'L0_attn_a_Wk': _L0_attn_a_in['Wk'], 'L0_attn_a_Wv': _L0_attn_a_in['Wv'], 'L0_attn_a_lambda_params': _L0_attn_a_in['lambda_params'], 'L0_attn_a_g1': _L0_attn_a_in['g1'], 'L0_attn_a_g2': _L0_attn_a_in['g2'], 'L0_attn_a_g3': _L0_attn_a_in['g3'], 'L0_attn_a_W1': _L0_attn_a_in['W1'], 'L0_attn_a_W2': _L0_attn_a_in['W2'], 'L0_attn_b_w_qkv': _L0_attn_b_in['w_qkv'], 'L0_attn_b_w_out': _L0_attn_b_in['w_out'], 'L0_attn_b_b_out': _L0_attn_b_in['b_out'], 'L0_ffn_gate_w': _L0_ffn_in['gate_w'], 'L0_ffn_gate_up_w': _L0_ffn_in['gate_up_w'], 'L0_ffn_down_w': _L0_ffn_in['down_w']}
    _x0 = _d['L0_attn_a_x']
    _d['L0_attn_a_x'] = jax.random.normal(jax.random.fold_in(jax.random.key(seed), 1), (4, 1024, 128), dtype=_x0.dtype)
    del _x0
    return _d

def reference(L0_attn_a_x, L0_attn_a_Wq, L0_attn_a_Wk, L0_attn_a_Wv, L0_attn_a_lambda_params, L0_attn_a_g1, L0_attn_a_g2, L0_attn_a_g3, L0_attn_a_W1, L0_attn_a_W2, L0_attn_b_w_qkv, L0_attn_b_w_out, L0_attn_b_b_out, L0_ffn_gate_w, L0_ffn_gate_up_w, L0_ffn_down_w):

    def _L0_attn_a_ref(x, Wq, Wk, Wv, lambda_params, g1, g2, g3, W1, W2):
        import jax, jax.numpy as jnp
        import numpy as np
        EPS = float(np.finfo(np.float32).eps)
        B, S, F_, E, H = (8, 512, 128, 128, 16)
        HD = E // H
        LAYER = 1
        LAMBDA_INIT = 0.8 - 0.6 * float(np.exp(-0.3 * (LAYER - 1)))
        SCALE = 1.0 / float(np.sqrt(E // 2))

        def _rms(x, g):
            return x * jax.lax.rsqrt(jnp.mean(x * x, axis=-1, keepdims=True) + EPS) * g
        b, s_len, _ = x.shape
        xn = _rms(x, g1)
        Q = jnp.einsum('bsf,ef->bse', xn, Wq).reshape(b, s_len, H, HD)
        K = jnp.einsum('bsf,ef->bse', xn, Wk).reshape(b, s_len, H, HD)
        V = jnp.einsum('bsf,ef->bse', xn, Wv).reshape(b, s_len, H, HD)
        pQ = jax.nn.elu(Q)
        pK = jax.nn.elu(K)
        Q1, Q2 = jnp.split(pQ, 2, axis=-1)
        K1, K2 = jnp.split(pK, 2, axis=-1)
        kv1 = jnp.einsum('bshe,bshd->bsed', K1, V) * SCALE
        kv2 = jnp.einsum('bshe,bshd->bsed', K2, V) * SCALE
        w1 = jnp.einsum('bshe,bsed->bshd', Q1, kv1)
        w2 = jnp.einsum('bshe,bsed->bshd', Q2, kv2)
        lmb = jnp.exp(lambda_params[0] * lambda_params[1]) - jnp.exp(lambda_params[2] * lambda_params[3]) + LAMBDA_INIT
        attn = w1 - lmb * w2
        attn = (1.0 - LAMBDA_INIT) * _rms(attn, g2)
        attn = attn.reshape(b, s_len, E)
        attn = _rms(attn, g3) + attn
        h = jax.nn.gelu(jnp.einsum('bse,fe->bsf', attn, W1), approximate=False)
        out = jnp.einsum('bsf,ef->bse', h, W2) + attn
        return out

    def _L0_attn_b_ref(x, w_qkv, w_out, b_out):
        import jax, jax.numpy as jnp
        import numpy as np
        B, S, D_IN = (2, 256, 128)
        D_OUT, H, WINDOW = (128, 16, 64)
        HD = D_OUT // H
        b, s, _ = x.shape
        qkv = jnp.einsum('bsi,oi->bso', x, w_qkv)
        q, k, v = jnp.split(qkv, 3, axis=-1)

        def heads(t):
            return t.reshape(b, s, H, HD).transpose(0, 2, 1, 3)
        q, k, v = (heads(q), heads(k), heads(v))
        scores = jnp.einsum('bhqd,bhkd->bhqk', q, k) / jnp.sqrt(jnp.asarray(HD, x.dtype))
        i = jnp.arange(s)[:, None]
        j = jnp.arange(s)[None, :]
        allowed = (j <= i) & (i - j < WINDOW)
        scores = jnp.where(allowed[None, None], scores, jnp.asarray(-jnp.inf, x.dtype))
        attn = jax.nn.softmax(scores, axis=-1)
        ctx = jnp.einsum('bhqk,bhkd->bhqd', attn, v)
        ctx = ctx.transpose(0, 2, 1, 3).reshape(b, s, D_OUT)
        return jnp.einsum('bso,po->bsp', ctx, w_out) + b_out

    def _L0_ffn_ref(hidden_states, gate_w, gate_up_w, down_w):
        import jax, jax.numpy as jnp
        import numpy as np
        TOP_K = 8
        NUM_EXPERTS = 32
        HIDDEN = 128
        EXPERT_DIM = 64
        B, S, H = hidden_states.shape
        x = hidden_states.reshape(-1, H)
        logits = x @ gate_w.T
        probs = jax.nn.softmax(logits.astype(jnp.float32), axis=-1)
        top_w, top_idx = jax.lax.top_k(probs, TOP_K)
        top_w = top_w / jnp.sum(top_w, axis=-1, keepdims=True)
        top_w = top_w.astype(x.dtype)
        comb = jnp.sum(jax.nn.one_hot(top_idx, NUM_EXPERTS, dtype=x.dtype) * top_w[..., None], axis=1)

        def body(acc, ws):
            guw, dw, w_e = ws
            gu = x @ guw.T
            g, u = jnp.split(gu, 2, axis=-1)
            y = u * jax.nn.silu(g) @ dw.T
            return (acc + y * w_e[:, None], None)
        init = jnp.zeros_like(x)
        out, _ = jax.lax.scan(body, init, (gate_up_w, down_w, comb.T))
        return out.reshape(B, S, H)
    x = L0_attn_a_x
    x = x + _L0_attn_a_ref(_layernorm(x, axis=-1), L0_attn_a_Wq, L0_attn_a_Wk, L0_attn_a_Wv, L0_attn_a_lambda_params, L0_attn_a_g1, L0_attn_a_g2, L0_attn_a_g3, L0_attn_a_W1, L0_attn_a_W2)
    x = x + _L0_ffn_ref(_layernorm(x, axis=-1), L0_ffn_gate_w, L0_ffn_gate_up_w, L0_ffn_down_w)
    x = x + _L0_attn_b_ref(_layernorm(x, axis=-1), L0_attn_b_w_qkv, L0_attn_b_w_out, L0_attn_b_b_out)
    x = x + _L0_ffn_ref(_layernorm(x, axis=-1), L0_ffn_gate_w, L0_ffn_gate_up_w, L0_ffn_down_w)
    return x

_drawn_inputs = setup_inputs


def setup_inputs(seed=0):
    import zlib

    import numpy as np

    out = dict(_drawn_inputs(seed))
    spreads = {'L0_attn_a_lambda_params': (0.800000011920929, 0.2),
     'L0_attn_a_g1': (1.0, 0.2),
     'L0_attn_a_g2': (1.0, 0.2),
     'L0_attn_a_g3': (1.0, 0.2)}
    factors = {'L0_ffn_gate_w': 8.0, 'L0_ffn_gate_up_w': 8.0, 'L0_ffn_down_w': 8.0}
    for name, (base, spread) in spreads.items():
        noise = np.random.default_rng([zlib.crc32(name.encode()), seed]).standard_normal(out[name].shape)
        drawn = base * np.exp(spread * noise) if base else spread * noise
        out[name] = jnp.asarray(drawn.astype(out[name].dtype))
    for name, factor in factors.items():
        out[name] = (out[name] * factor).astype(out[name].dtype)
    return out
```

```python
from contextlib import ExitStack

import numpy as np

import concourse.bass as bass
from concourse import mybir

F32 = mybir.dt.float32
F32R = mybir.dt.float32r
BF16 = mybir.dt.bfloat16
I32 = mybir.dt.int32
ALU = mybir.AluOpType
ACT = mybir.ActivationFunctionType
AX_X = mybir.AxisListType.X

P = 128
ROWS, SEQ, D = 4, 1024, 128
T = 4
GT = T * P
G = SEQ // GT
TILES = SEQ // P
STAGES = 4 * G
H, HD = 16, 8
HALF = HD // 2
NE, ED = 32, 64
TOP = 8
CH = NE * ED // P
MOE = 2 * G
QB = 32
WIN = 64
KW = WIN + QB
HG = P // QB
NB = P // QB
NEG = -3.0e38
LN_EPS = 1e-5
RMS_EPS = float(np.finfo(np.float32).eps)
LAMBDA_INIT = 0.8 - 0.6 * float(np.exp(-0.3 * 0))
KV_SCALE = 1.0 / float(np.sqrt(D // 2))
Q_SCALE = 1.0 / float(np.sqrt(HD))
RSQRT_MAGIC = float(0x5F3759DF)
VECTOR_STEPS = 300
SCALAR_STEPS = 8


def hybrid_block(nc, x, wqkv_a, lam, g1, g2, g3, w1, w2, wqkv_b, wout, bout, wgate, wg, wu, wd, out):
    x_rows = x.rearrange("(r t p) d -> r p t d", r=ROWS, p=P)
    out_rows = out.rearrange("(r t p) d -> r p t d", r=ROWS, p=P)

    with ExitStack() as ctx:
        def sb(name, shape, dt=F32):
            return ctx.enter_context(nc.sbuf_tensor(name, shape, dt))

        def sem(name):
            return ctx.enter_context(nc.semaphore(name))

        qkv_a_w = sb("qkv_a_w", [P, 3 * D])
        w1_w, w2_w = sb("w1_w", [P, D]), sb("w2_w", [P, D])
        qkv_b_w, out_w = sb("qkv_b_w", [P, 3 * D]), sb("out_w", [P, D])
        bout_row = sb("bout_row", [1, D])
        router_w = sb("router_w", [P, NE])
        stage_w = sb("stage_w", [P, NE * ED])
        gate_hi, gate_lo = sb("gate_hi", [P, NE * ED], F32R), sb("gate_lo", [P, NE * ED], F32R)
        up_hi, up_lo = sb("up_hi", [P, NE * ED], F32R), sb("up_lo", [P, NE * ED], F32R)
        router_hi, router_lo = sb("router_hi", [P, NE], F32R), sb("router_lo", [P, NE], F32R)
        down_w = sb("down_w", [P, CH, D])
        g1_col, g2_row, g3_row = sb("g1_col", [P, 1]), sb("g2_row", [P, HD]), sb("g3_row", [P, D])
        lam_row, lam_prod, lam_exp = sb("lam_row", [P, 4]), sb("lam_prod", [P, 2]), sb("lam_exp", [P, 2])
        lam_diff = sb("lam_diff", [P, 1])
        kv_coef = sb("kv_coef", [P, HD * HD])
        ident, ident_bf = sb("ident", [P, P]), sb("ident_bf", [P, P], BF16)
        ones_row = sb("ones_row", [1, P])
        head_bits, head_mask = sb("head_bits", [P, HG, HG]), sb("head_mask", [P, HG])
        q_mask = sb("q_mask", [P, HG])
        window = sb("window", [P, 2, NB, KW], BF16)
        expert_sel = sb("expert_sel", [3 * NE, NE, ED], BF16)

        x_in, xs, x_out = (sb(n, [P, TILES, D]) for n in ("x_in", "xs", "x_out"))
        stats, moments = sb("stats", [P, T, 6]), sb("moments", [P, T, 2])
        rstd, msq, rms = sb("rstd", [P, T]), sb("msq", [P, T]), sb("rms", [P, T])
        z = sb("z", [P, T, D])
        zT = sb("zT", [P, GT])
        qkv = sb("qkv", [P, 2, 3 * D])
        eneg = sb("eneg", [P, 2, 2 * D])
        elu = sb("elu", [P, 2, 2 * D])
        kv_terms, w_terms = sb("kv_terms", [P, 2, HD * HD * H]), sb("w_terms", [P, H * HD * HD])
        kv = sb("kv", [P, HD * HD])
        attn, squares = sb("attn", [P, T, D]), sb("squares", [P, T, D])
        head_rms, tok_rms = sb("head_rms", [P, T * H]), sb("tok_rms", [P, T])
        wait_carrier = sb("wait_carrier", [P, 1])
        var_eps, newton = sb("var_eps", [P, T]), sb("newton", [P, T * H])
        head_ms, tok_ms = sb("head_ms", [P, T * H]), sb("tok_ms", [P, T])
        gain = sb("gain", [P, T, D])
        attn_sum = sb("attn_sum", [P, T, D])
        attnT, hidT = sb("attnT", [P, GT]), sb("hidT", [P, GT])
        z_hi, z_lo = sb("z_hi", [P, GT], F32R), sb("z_lo", [P, GT], F32R)
        logits, top, shifted = sb("logits", [P, T, NE]), sb("top", [P, T, TOP]), sb("shifted", [P, T, NE])
        expd, top_exp, replaced = sb("expd", [P, T, NE]), sb("top_exp", [P, T, TOP]), sb("replaced", [P, T, NE])
        top_sum, top_inv = sb("top_sum", [P, T]), sb("top_inv", [P, T])
        comb, comb_rest = sb("comb", [P, T, NE]), sb("comb_rest", [P, 2, T, NE])
        comb_parts = sb("comb_parts", [P, T, 3, NE], BF16)
        combT = sb("combT", [3 * NE, GT], BF16)
        silu, gated, hid = (sb(n, [P, 2, GT]) for n in ("silu", "gated", "hid"))
        yT = sb("yT", [P, GT])
        seqT, keysT = sb("seqT", [P, WIN + SEQ]), sb("keysT", [P, WIN + SEQ])
        qm = sb("qm", [P, NB * T, HG, QB])
        vals = sb("vals", [KW, 2, NB * D])
        neg_max, prob_sum, prob_inv = (sb(n, [P, 2, NB * HG]) for n in ("neg_max", "prob_sum", "prob_inv"))
        probs = sb("probs", [P, 2, NB * HG, KW])
        probsT = sb("probsT", [KW, NB, HG * P])
        mixT = sb("mixT", [P, T, P])
        mix_part = sb("mix_part", [P, 3, P])

        bank = [ctx.enter_context(nc.psum_tensor(f"bank{i}", [P, 512], F32)) for i in range(6)]
        sc4 = ctx.enter_context(nc.psum_tensor("bank67", [P, 2, 512], F32))
        bank += [sc4[:, 0, :], sc4[:, 1, :]]

        weights_in, x_loaded, x_stored = sem("weights_in"), sem("x_loaded"), sem("x_stored")
        pool_const, const_ready, setup_step = sem("pool_const"), sem("const_ready"), sem("setup_step")
        vector_step, scalar_step = sem("vector_step"), sem("scalar_step")
        z_ready, zT_ready, zT_copied = sem("z_ready"), sem("zT_ready"), sem("zT_copied")
        residual_done = sem("residual_done")
        qkv_ready, qkv_taken, eneg_ready = sem("qkv_ready"), sem("qkv_taken"), sem("eneg_ready")
        elu_ready, kv_terms_ready, kv_summed = sem("elu_ready"), sem("kv_terms_ready"), sem("kv_summed")
        attn_ready, attn_added, attnT_ready = sem("attn_ready"), sem("attn_added"), sem("attnT_ready")
        attnT_copied, hid_ready, gelu_ready, mlp_ready = (
            sem("attnT_copied"), sem("hid_ready"), sem("gelu_ready"), sem("mlp_ready"))
        zlo_ready, logits_ready, shifted_ready, expd_ready = (
            sem("zlo_ready"), sem("logits_ready"), sem("shifted_ready"), sem("expd_ready"))
        comb_ready, combT_ready, combT_copied = sem("comb_ready"), sem("combT_ready"), sem("combT_copied")
        gate_ready, up_ready, spread_ready = sem("gate_ready"), sem("up_ready"), sem("spread_ready")
        silu_ready, gated_ready, hid_gated, down_done = (
            sem("silu_ready"), sem("gated_ready"), sem("hid_gated"), sem("down_done"))
        y_copied, y_turned = sem("y_copied"), sem("y_turned")
        q_ready, k_ready, q_masked, k_copied = sem("q_ready"), sem("k_ready"), sem("q_masked"), sem("k_copied")
        v_ready, v_copied, scores_ready, max_ready = (
            sem("v_ready"), sem("v_copied"), sem("scores_ready"), sem("max_ready"))
        probs_ready, inv_ready, probs_normed = sem("probs_ready"), sem("inv_ready"), sem("probs_normed")
        probsT_ready, probsT_by_act, probsT_by_dve = (
            sem("probsT_ready"), sem("probsT_by_act"), sem("probsT_by_dve"))
        mix_ready, mix_picked, proj_ready = sem("mix_ready"), sem("mix_picked"), sem("proj_ready")

        loads = [(qkv_a_w[:], wqkv_a), (w1_w[:], w1), (w2_w[:], w2), (qkv_b_w[:], wqkv_b), (out_w[:], wout),
                 (bout_row[:], bout.rearrange("(a n) -> a n", a=1)), (router_w[:], wgate),
                 (down_w[:], wd.rearrange("(c p) d -> p c d", p=P)),
                 (g1_col[:], g1.rearrange("(p a) -> p a", a=1)), (g2_row[:], g2.partition_broadcast(P)),
                 (g3_row[:], g3.partition_broadcast(P)), (lam_row[:], lam.partition_broadcast(P))]
        N_LOADS = len(loads)

        def after(row, per_row, n):
            return row * per_row + max(n, 0) + 1

        block = ctx.enter_context(nc.Block())

        @block.sync
        def _(sp):
            for started in (attnT_copied, attnT_ready, attn_added, attn_ready, combT_copied, combT_ready, comb_ready, down_done,
                      elu_ready, eneg_ready, expd_ready, gate_ready, gated_ready, gelu_ready, hid_gated, hid_ready,
                      inv_ready, k_copied, k_ready, kv_summed, kv_terms_ready, logits_ready, max_ready, mix_picked,
                      mix_ready, mlp_ready, probsT_by_act, probsT_by_dve, probsT_ready, probs_normed, probs_ready,
                      proj_ready, q_masked, q_ready, qkv_ready, residual_done, scores_ready, shifted_ready, silu_ready,
                      spread_ready, up_ready, v_copied, v_ready, x_loaded, x_stored, y_copied, y_turned, zT_copied,
                      zT_ready, z_ready, zlo_ready):
                sp.sem_inc(started, 1)
            for dst, src in loads:
                sp.dma_start(dst, src).then_inc(weights_in, 16)
            sp.dma_start(stage_w[:], wg).then_inc(weights_in, 16)
            sp.wait_ge(const_ready, 2)
            sp.dma_start(stage_w[:], wu).then_inc(weights_in, 16)
            with sp.Fori(0, ROWS) as row:
                sp.wait_ge(attn_added, after(row, G, 0))
                sp.dma_start(x_in[:], x_rows[row]).then_inc(x_loaded, 16)
                sp.wait_ge(residual_done, after(row, STAGES, STAGES))
                sp.dma_start(out_rows[row], x_out[:]).then_inc(x_stored, 16)
            sp.wait_ge(x_stored, ROWS * 16 + 1)

        @block.gpsimd
        def _(pool):
            n = [0]

            def step(ins):
                n[0] += 1
                ins.then_inc(pool_const, 1)
                pool.wait_ge(pool_const, n[0])

            step(pool.memset(ident[:], 0.0))
            step(pool.memset(ident_bf[:], 0.0))
            for t in (ident, ident_bf):
                step(pool.affine_select(out=t[:], in_=t[:], compare_op=ALU.not_equal, fill=1.0, base=0,
                                        pattern=[[-1, P]], channel_multiplier=1))
            step(pool.memset(ones_row[:], 1.0))
            step(pool.memset(head_bits[:], 1.0))
            step(pool.affine_select(out=head_bits[:], in_=head_bits[:], compare_op=ALU.is_ge, fill=0.0, base=0,
                                    pattern=[[-HG * HD, HG], [-HD, HG]], channel_multiplier=1))
            step(pool.affine_select(out=head_bits[:], in_=head_bits[:], compare_op=ALU.is_ge, fill=0.0,
                                    base=HD - 1, pattern=[[HG * HD, HG], [HD, HG]], channel_multiplier=-1))
            step(pool.memset(window[:], 0.0))
            for j in range(HG):
                rows = window[QB * j:QB * (j + 1)]
                step(pool.affine_select(out=rows, in_=rows, compare_op=ALU.is_gt, fill=NEG, base=0,
                                        pattern=[[0, 2], [0, NB], [1, KW]], channel_multiplier=-1))
                step(pool.affine_select(out=rows, in_=rows, compare_op=ALU.is_ge, fill=NEG, base=WIN,
                                        pattern=[[0, 2], [0, NB], [-1, KW]], channel_multiplier=1))
            for b in range(WIN // QB):
                step(pool.memset(window[:, 0, b, 0:WIN - QB * b], NEG))
            step(pool.memset(expert_sel[:], 0.0))
            for part in range(3):
                step(pool.affine_select(out=expert_sel[:], in_=expert_sel[:], compare_op=ALU.not_equal,
                                        fill=1.0, base=-NE * part, pattern=[[-1, NE], [0, ED]],
                                        channel_multiplier=1))
            step(pool.memset(seqT[:, 0:WIN], 0.0))
            step(pool.memset(keysT[:, 0:WIN], 0.0))
            pool.memset(kv_coef[:], KV_SCALE).then_inc(const_ready, 1)

            with pool.Fori(0, ROWS) as row:
                for g in range(G):
                    for t in range(T):
                        i = T * g + t
                        pool.wait_ge(elu_ready, after(row, TILES, i + 1))
                        pool.wait_ge(kv_summed, after(row, TILES, i - 1))
                        k = elu[:, t % 2, D:2 * D].rearrange("p (h e) -> p e h", e=HD)
                        v = qkv[:, t % 2, 2 * D:3 * D].rearrange("p (h d) -> p d h", d=HD)
                        pool.tensor_tensor(
                            kv_terms[:, t % 2].rearrange("p (e d h) -> p e d h", e=HD, d=HD),
                            k.unsqueeze(2).broadcast_to([P, HD, HD, H]),
                            v.unsqueeze(1).broadcast_to([P, HD, HD, H]), ALU.mult).then_inc(kv_terms_ready, 1)
                    pool.wait_ge(attn_ready, after(row, G, g + 1))
                    pool.wait_ge(x_loaded, after(row, 16, 16))
                    if g == 0:
                        pool.wait_ge(residual_done, after(row, STAGES, 0))
                    pool.tensor_tensor(xs[:, T * g:T * g + T], x_in[:, T * g:T * g + T], attn_sum[:],
                                       ALU.add).then_inc(attn_added, 1)
                for i in range(TILES):
                    pool.wait_ge(inv_ready, after(row, TILES, i + 1))
                    pr = probs[:, i % 2]
                    pool.tensor_tensor(pr, pr, prob_inv[:, i % 2].unsqueeze(2).broadcast_to([P, NB * HG, KW]),
                                       ALU.mult).then_inc(probs_normed, 1)

        @block.scalar
        def _(act):
            act.wait_ge(weights_in, 16 * (N_LOADS + 1))
            act.wait_ge(setup_step, 1)
            act.activation(lam_exp[:], lam_prod[:], ACT.Exp).then_inc(setup_step, 1)

            with act.Fori(0, ROWS) as row:
                n_step = [0]

                def step(ins):
                    n_step[0] += 1
                    ins.then_inc(scalar_step, 1)
                    act.wait_ge(scalar_step, row * SCALAR_STEPS + n_step[0])

                for g in range(G):
                    act.wait_ge(zT_ready, after(row, STAGES, g + 1))
                    act.wait_ge(qkv_ready, after(row, TILES, T * g))
                    act.activation(zT[:], bank[7], ACT.Copy).then_inc(zT_copied, 1)
                    for t in range(T):
                        i = T * g + t
                        act.wait_ge(qkv_ready, after(row, TILES, i + 1))
                        act.wait_ge(kv_terms_ready, after(row, TILES, i - 1))
                        act.activation(qkv[:, t % 2], bank[t % 2][:, 0:3 * D], ACT.Copy)
                        step(act.activation(eneg[:, t % 2], bank[t % 2][:, 0:2 * D], ACT.Relu, scale=-1.0))
                        act.activation(eneg[:, t % 2], eneg[:, t % 2], ACT.Exp, scale=-1.0).then_inc(eneg_ready, 1)
                    act.wait_ge(attnT_ready, after(row, G, g + 1))
                    act.activation(attnT[:], bank[6], ACT.Copy).then_inc(attnT_copied, 1)
                    act.wait_ge(hid_ready, after(row, G, g + 1))
                    act.activation(hidT[:], bank[5][:], ACT.Gelu).then_inc(gelu_ready, 1)

                def experts(f, k):
                    act.wait_ge(zT_ready, after(row, STAGES, k + 1))
                    act.wait_ge(up_ready, after(row, MOE * CH, f * CH))
                    act.activation(z_hi[:], bank[7], ACT.Copy).then_inc(zT_copied, 1)
                    act.wait_ge(shifted_ready, after(row, MOE, f + 1))
                    act.activation(expd[:], shifted[:], ACT.Exp).then_inc(expd_ready, 1)
                    for c in range(CH):
                        if c == 2:
                            act.wait_ge(combT_ready, after(row, MOE, f + 1))
                            act.activation(combT[:], bank[7][0:3 * NE, 0:GT // 2].bitcast(BF16),
                                           ACT.Copy).then_inc(combT_copied, 1)
                        n = f * CH + c
                        act.wait_ge(gate_ready, after(row, MOE * CH, n + 1))
                        act.wait_ge(gated_ready, after(row, MOE * CH, n - 1))
                        act.activation(silu[:, c % 2], bank[c % 2][:], ACT.Silu).then_inc(silu_ready, 1)
                    act.wait_ge(down_done, after(row, MOE * CH, f * CH + CH))
                    act.activation(yT[:], bank[6], ACT.Copy).then_inc(y_copied, 1)

                for g in range(G):
                    experts(g, G + g)

                for g in range(G):
                    act.wait_ge(zT_ready, after(row, STAGES, 2 * G + g + 1))
                    act.activation(seqT[:, WIN + GT * g:WIN + GT * (g + 1)], bank[7], ACT.Copy).then_inc(zT_copied, 1)
                    act.wait_ge(q_ready, after(row, G, g + 1))
                    act.wait_ge(scores_ready, after(row, TILES, T * g))
                    for j in range(HG):
                        a = act.activation(qm[:, :, j, :], bank[6].rearrange("p (b q) -> p b q", q=QB),
                                           ACT.Copy, scale=q_mask[:, j:j + 1])
                    a.then_inc(q_masked, 1)
                    act.wait_ge(k_ready, after(row, G, g + 1))
                    act.activation(keysT[:, WIN + GT * g:WIN + GT * (g + 1)], bank[7], ACT.Copy).then_inc(k_copied, 1)

                    def transposed(i):
                        for b in range(0, NB, 2):
                            act.wait_ge(probsT_ready, after(row, TILES * NB, i * NB + b + 1))
                            act.wait_ge(mix_ready, after(row, TILES, i))
                            act.activation(probsT[:, b], bank[4 + b % 2][0:KW, :], ACT.Copy).then_inc(probsT_by_act, 1)

                    for t in range(T):
                        i = T * g + t
                        act.wait_ge(v_ready, after(row, TILES, i + 1))
                        act.wait_ge(mix_ready, after(row, TILES, i - 1))
                        act.activation(vals[:, i % 2], bank[7][0:KW, :], ACT.Copy).then_inc(v_copied, 1)
                        act.wait_ge(max_ready, after(row, TILES, i + 1))
                        act.wait_ge(probsT_ready, after(row, TILES * NB, (i - 1) * NB))
                        for hg in range(HG):
                            for b in range(NB):
                                m = hg * NB + b
                                a = act.activation(probs[:, i % 2, m], bank[hg][:, b * KW:(b + 1) * KW], ACT.Exp,
                                                   bias=neg_max[:, i % 2, m:m + 1],
                                                   accum_out=prob_sum[:, i % 2, m:m + 1])
                        a.then_inc(probs_ready, 1)
                        if t:
                            transposed(i - 1)
                    transposed(T * g + T - 1)

                for g in range(G):
                    experts(G + g, 3 * G + g)
                assert n_step[0] == SCALAR_STEPS, n_step[0]

        @block.vector
        def _(dve):
            dve.wait_ge(weights_in, 16 * (N_LOADS + 1))
            dve.wait_ge(pool_const, 1)
            dve.tensor_scalar(qkv_a_w[:], qkv_a_w[:], g1_col[:, 0:1], None, ALU.mult)
            dve.tensor_copy(gate_hi[:], stage_w[:])
            dve.tensor_copy(router_hi[:], router_w[:])
            dve.tensor_tensor(lam_prod[:], lam_row[:, 0:4:2], lam_row[:, 1:4:2], ALU.mult).then_inc(setup_step, 1)
            dve.wait_ge(setup_step, 2)
            dve.tensor_tensor(gate_lo[:], stage_w[:], gate_hi[:], ALU.subtract).then_inc(const_ready, 1)
            dve.tensor_tensor(router_lo[:], router_w[:], router_hi[:], ALU.subtract)
            dve.wait_ge(weights_in, 16 * (N_LOADS + 2))
            dve.tensor_copy(up_hi[:], stage_w[:]).then_inc(setup_step, 1)
            dve.wait_ge(setup_step, 3)
            dve.tensor_tensor(up_lo[:], stage_w[:], up_hi[:], ALU.subtract).then_inc(setup_step, 1)
            dve.tensor_tensor(lam_diff[:], lam_exp[:, 0:1], lam_exp[:, 1:2], ALU.subtract).then_inc(setup_step, 1)
            dve.wait_ge(setup_step, 5)
            dve.tensor_scalar(lam_diff[:], lam_diff[:], LAMBDA_INIT, -1.0, ALU.add, ALU.mult).then_inc(setup_step, 1)
            dve.wait_ge(setup_step, 6)
            dve.wait_ge(const_ready, 2)
            dve.tensor_scalar(kv_coef[:, HALF * HD:], kv_coef[:, HALF * HD:], lam_diff[:, 0:1], None, ALU.mult)
            dve.tensor_scalar(g2_row[:], g2_row[:], 1.0 - LAMBDA_INIT, None, ALU.mult)
            dve.tensor_reduce(head_mask[:], head_bits[:].rearrange("p g j -> p j g"), AX_X, ALU.add).then_inc(setup_step, 1)
            dve.wait_ge(setup_step, 7)
            dve.tensor_scalar(q_mask[:], head_mask[:], Q_SCALE, None, ALU.mult).then_inc(const_ready, 1)
            dve.wait_ge(const_ready, 3)

            with dve.Fori(0, ROWS) as row:
                n_step = [0]

                def mark(ins):
                    n_step[0] += 1
                    ins.then_inc(vector_step, 1)

                def settle():
                    dve.wait_ge(vector_step, row * VECTOR_STEPS + n_step[0])

                def step(ins):
                    mark(ins)
                    settle()

                def carry():
                    dve.memset(wait_carrier[:], 0.0)

                def inv_sqrt(y, v, tmp):
                    step(dve.tensor_single_scalar(tmp.bitcast(I32), v.bitcast(I32), 1, ALU.arith_shift_right))
                    step(dve.tensor_scalar(y.bitcast(I32), tmp.bitcast(I32), -1.0, RSQRT_MAGIC, ALU.mult, ALU.add))
                    for _ in range(3):
                        step(dve.tensor_tensor(tmp, y, y, ALU.mult))
                        step(dve.scalar_tensor_tensor(out=tmp, in0=tmp, scalar=-0.5, in1=v, op0=ALU.mult,
                                                      op1=ALU.mult))
                        step(dve.scalar_tensor_tensor(out=y, in0=tmp, scalar=1.5, in1=y, op0=ALU.add,
                                                      op1=ALU.mult))

                def norm(src, g, k, with_rms):
                    for t in range(T):
                        ins = dve.bn_stats(stats[:, t], src[:, T * g + t])
                    step(ins)
                    carry()
                    for t in range(T):
                        ins = dve.bn_aggr(moments[:, t], stats[:, t])
                    step(ins)
                    step(dve.tensor_scalar(var_eps[:], moments[:, :, 1], LN_EPS, None, ALU.add))
                    inv_sqrt(rstd[:], var_eps[:], newton[:, 0:T])
                    if with_rms:
                        step(dve.tensor_tensor(msq[:], rstd[:], rstd[:], ALU.mult))
                        step(dve.tensor_tensor(msq[:], msq[:], moments[:, :, 1], ALU.mult))
                        step(dve.tensor_scalar(msq[:], msq[:], RMS_EPS, None, ALU.add))
                        inv_sqrt(rms[:], msq[:], newton[:, 0:T])
                        step(dve.tensor_tensor(rstd[:], rstd[:], rms[:], ALU.mult))
                    dve.wait_ge(zT_ready, after(row, STAGES, k))
                    for t in range(T):
                        ins = dve.tensor_scalar(z[:, t], src[:, T * g + t], moments[:, t, 0:1], rstd[:, t:t + 1],
                                                ALU.subtract, ALU.mult)
                    ins.then_inc(z_ready, 1)

                def elus(i):
                    dve.wait_ge(eneg_ready, after(row, TILES, i + 1))
                    dve.wait_ge(kv_terms_ready, after(row, TILES, i - 1))
                    dve.scalar_tensor_tensor(out=elu[:, i % 2], in0=eneg[:, i % 2], scalar=-1.0,
                                             in1=qkv[:, i % 2, 0:2 * D], op0=ALU.add, op1=ALU.max)\
                       .then_inc(elu_ready, 1)

                def attend(i):
                    dve.wait_ge(kv_terms_ready, after(row, TILES, i + 1))
                    dve.tensor_reduce(kv[:], kv_terms[:, i % 2].rearrange("p (c h) -> p c h", h=H), AX_X,
                                      ALU.add).then_inc(kv_summed, 1)
                    dve.wait_ge(kv_summed, after(row, TILES, i + 1))
                    step(dve.tensor_tensor(kv[:], kv[:], kv_coef[:], ALU.mult))
                    q = elu[:, i % 2, 0:D].rearrange("p (h e) -> p h e", e=HD)
                    kvT = kv[:].rearrange("p (e d) -> p d e", d=HD)
                    step(dve.tensor_tensor(w_terms[:].rearrange("p (h d e) -> p h d e", h=H, d=HD),
                                           q.unsqueeze(2).broadcast_to([P, H, HD, HD]),
                                           kvT.unsqueeze(1).broadcast_to([P, H, HD, HD]), ALU.mult))
                    mark(dve.tensor_reduce(attn[:, i % T], w_terms[:].rearrange("p (c e) -> p c e", e=HD), AX_X,
                                           ALU.add))

                for g in range(G):
                    dve.wait_ge(x_loaded, after(row, 16, 16))
                    norm(x_in, g, g, True)
                    elus(T * g)
                    for t in range(T):
                        if t + 1 < T:
                            elus(T * g + t + 1)
                        attend(T * g + t)
                    settle()
                    flat = "p t (h d) -> p (t h) d"
                    a3 = attn[:].rearrange(flat, d=HD)
                    step(dve.tensor_tensor(squares[:], attn[:], attn[:], ALU.mult))
                    step(dve.tensor_reduce(head_ms[:], squares[:].rearrange(flat, d=HD), AX_X, ALU.add))
                    step(dve.tensor_scalar(head_ms[:], head_ms[:], 1.0 / HD, RMS_EPS, ALU.mult, ALU.add))
                    inv_sqrt(head_rms[:], head_ms[:], newton[:])
                    step(dve.tensor_tensor(a3, a3, head_rms[:].unsqueeze(2).broadcast_to([P, T * H, HD]), ALU.mult))
                    step(dve.tensor_tensor(a3, a3, g2_row[:].unsqueeze(1).broadcast_to([P, T * H, HD]), ALU.mult))
                    step(dve.tensor_tensor(squares[:], attn[:], attn[:], ALU.mult))
                    step(dve.tensor_reduce(tok_ms[:], squares[:], AX_X, ALU.add))
                    step(dve.tensor_scalar(tok_ms[:], tok_ms[:], 1.0 / D, RMS_EPS, ALU.mult, ALU.add))
                    inv_sqrt(tok_rms[:], tok_ms[:], newton[:, 0:T])
                    for t in range(T):
                        ins = dve.tensor_scalar(gain[:, t], g3_row[:], tok_rms[:, t:t + 1], 1.0, ALU.mult, ALU.add)
                    step(ins)
                    dve.wait_ge(attnT_ready, after(row, G, g))
                    dve.wait_ge(attn_added, after(row, G, g))
                    dve.tensor_tensor(attn_sum[:], attn[:], gain[:], ALU.mult).then_inc(attn_ready, 1)
                    dve.wait_ge(mlp_ready, after(row, G, g + 1))
                    dve.wait_ge(attn_added, after(row, G, g + 1))
                    xg = xs[:, T * g:T * g + T].rearrange("p t d -> p (t d)")
                    dve.tensor_tensor(xg, xg, bank[4][:], ALU.add).then_inc(residual_done, 1)

                def experts(f, g, k, dst):
                    dve.wait_ge(residual_done, after(row, STAGES, k - G + 1))
                    norm(xs, g, k, False)
                    dve.wait_ge(zT_copied, after(row, STAGES, k + 1))
                    dve.wait_ge(up_ready, after(row, MOE * CH, f * CH))
                    dve.tensor_tensor(z_lo[:], bank[7], z_hi[:], ALU.subtract).then_inc(zlo_ready, 1)
                    dve.wait_ge(logits_ready, after(row, MOE, f + 1))
                    step(dve.tensor_copy(logits[:].rearrange("p t e -> p (t e)"), bank[7][:, 0:T * NE]))
                    carry()
                    for t in range(T):
                        ins = dve.max(top[:, t], logits[:, t])
                    step(ins)
                    dve.tensor_tensor(shifted[:], logits[:], top[:, :, 0:1].broadcast_to([P, T, NE]),
                                      ALU.subtract).then_inc(shifted_ready, 1)
                    dve.wait_ge(expd_ready, after(row, MOE, f + 1))
                    carry()
                    for t in range(T):
                        ins = dve.max(top_exp[:, t], expd[:, t])
                    step(ins)
                    carry()
                    for t in range(T):
                        ins = dve.match_replace(replaced[:, t], top_exp[:, t], expd[:, t], -1.0)
                    mark(ins)
                    step(dve.tensor_reduce(top_sum[:], top_exp[:], AX_X, ALU.add))
                    mark(dve.reciprocal(top_inv[:], top_sum[:]))
                    step(dve.scalar_tensor_tensor(out=comb[:], in0=replaced[:], scalar=0.0, in1=expd[:],
                                                  op0=ALU.is_lt, op1=ALU.mult))
                    step(dve.tensor_tensor(comb[:], comb[:], top_inv[:].unsqueeze(2).broadcast_to([P, T, NE]),
                                           ALU.mult))
                    dve.wait_ge(combT_ready, after(row, MOE, f))
                    step(dve.tensor_copy(comb_parts[:, :, 0], comb[:]))
                    step(dve.tensor_tensor(comb_rest[:, 0], comb[:], comb_parts[:, :, 0], ALU.subtract))
                    step(dve.tensor_copy(comb_parts[:, :, 1], comb_rest[:, 0]))
                    step(dve.tensor_tensor(comb_rest[:, 1], comb_rest[:, 0], comb_parts[:, :, 1], ALU.subtract))
                    dve.tensor_copy(comb_parts[:, :, 2], comb_rest[:, 1]).then_inc(comb_ready, 1)

                    def gate(c):
                        n = f * CH + c
                        dve.wait_ge(silu_ready, after(row, MOE * CH, n + 1))
                        dve.wait_ge(up_ready, after(row, MOE * CH, n + 1))
                        dve.wait_ge(hid_gated, after(row, MOE * CH, n - 1))
                        dve.tensor_tensor(gated[:, c % 2], silu[:, c % 2], bank[2 + c % 2][:], ALU.mult)\
                           .then_inc(gated_ready, 1)

                    gate(0)
                    for c in range(CH):
                        n = f * CH + c
                        if c + 1 < CH:
                            gate(c + 1)
                        dve.wait_ge(gated_ready, after(row, MOE * CH, n + 1))
                        dve.wait_ge(spread_ready, after(row, MOE * CH, n + 1))
                        dve.wait_ge(down_done, after(row, MOE * CH, n - 1))
                        dve.tensor_tensor(hid[:, c % 2], gated[:, c % 2], bank[4 + c % 2][:], ALU.mult)\
                           .then_inc(hid_gated, 1)
                    dve.wait_ge(y_turned, after(row, MOE, f + 1))
                    if dst is x_out:
                        dve.wait_ge(x_stored, after(row, 16, 0))
                    flat = "p t d -> p (t d)"
                    dve.tensor_tensor(dst[:, T * g:T * g + T].rearrange(flat), xs[:, T * g:T * g + T].rearrange(flat),
                                      bank[7], ALU.add).then_inc(residual_done, 1)

                for g in range(G):
                    experts(g, g, G + g, xs)

                for g in range(G):
                    dve.wait_ge(residual_done, after(row, STAGES, G + g + 1))
                    norm(xs, g, 2 * G + g, False)

                    def finish(i):
                        for b in range(1, NB, 2):
                            dve.wait_ge(probsT_ready, after(row, TILES * NB, i * NB + b + 1))
                            dve.wait_ge(mix_ready, after(row, TILES, i))
                            dve.tensor_copy(probsT[:, b], bank[4 + b % 2][0:KW, :]).then_inc(probsT_by_dve, 1)
                        dve.wait_ge(mix_ready, after(row, TILES, i + 1))
                        if i % T == 0:
                            dve.wait_ge(proj_ready, after(row, G, i // T))
                        mix = bank[6].rearrange("p (b j q) -> p j b q", b=NB, j=HG)
                        part = lambda a: a.rearrange("p (b q) -> p b q", q=QB)
                        step(dve.tensor_scalar(part(mix_part[:, 0]), mix[:, 0], head_mask[:, 0:1], None, ALU.mult))
                        for j in range(1, HG):
                            dst = part(mix_part[:, j]) if j < HG - 1 else part(mixT[:, i % T])
                            ins = dve.scalar_tensor_tensor(out=dst, in0=mix[:, j], scalar=head_mask[:, j:j + 1],
                                                           in1=part(mix_part[:, j - 1]), op0=ALU.mult, op1=ALU.add)
                            if j < HG - 1:
                                step(ins)
                            else:
                                ins.then_inc(mix_picked, 1)

                    for t in range(T):
                        i = T * g + t
                        dve.wait_ge(scores_ready, after(row, TILES, i + 1))
                        dve.wait_ge(probs_ready, after(row, TILES, i - 1))
                        for hg in range(HG):
                            ins = dve.tensor_reduce(neg_max[:, i % 2, hg * NB:(hg + 1) * NB],
                                                    bank[hg][:, 0:NB * KW].rearrange("p (b k) -> p b k", k=KW),
                                                    AX_X, ALU.max, negate=True)
                        ins.then_inc(max_ready, 1)
                        if t:
                            finish(i - 1)
                        dve.wait_ge(probs_ready, after(row, TILES, i + 1))
                        dve.reciprocal(prob_inv[:, i % 2], prob_sum[:, i % 2]).then_inc(inv_ready, 1)
                    finish(T * g + T - 1)
                    dve.wait_ge(proj_ready, after(row, G, g + 1))
                    xg = xs[:, T * g:T * g + T].rearrange("p t d -> p (t d)")
                    dve.tensor_tensor(xg, xg, bank[7], ALU.add).then_inc(residual_done, 1)

                for g in range(G):
                    experts(G + g, g, 3 * G + g, x_out)
                assert n_step[0] == VECTOR_STEPS, n_step[0]

        @block.tensor
        def _(pe):
            pe.wait_ge(const_ready, 3)
            pe.wait_ge(setup_step, 7)

            with pe.Fori(0, ROWS) as row:
                def turn(k):
                    pe.wait_ge(z_ready, after(row, STAGES, k + 1))
                    pe.wait_ge(residual_done, after(row, STAGES, k if k % G == 0 or k >= G else 0))
                    for t in range(T):
                        mm = pe.transpose(bank[7][:, P * t:P * (t + 1)], z[:, t], ident[:])
                    mm.then_inc(zT_ready, 1)

                for g in range(G):
                    if g:
                        pe.wait_ge(zT_copied, after(row, STAGES, g))
                    turn(g)
                    pe.wait_ge(zT_copied, after(row, STAGES, g + 1))
                    for t in range(T):
                        i = T * g + t
                        pe.wait_ge(eneg_ready, after(row, TILES, i - 1))
                        pe.matmul(bank[t % 2][:, 0:3 * D], zT[:, P * t:P * (t + 1)], qkv_a_w[:],
                                  start=True, stop=True).then_inc(qkv_ready, 1)
                    pe.wait_ge(attn_ready, after(row, G, g + 1))
                    for t in range(T):
                        mm = pe.transpose(bank[6][:, P * t:P * (t + 1)], attn_sum[:, t], ident[:])
                    mm.then_inc(attnT_ready, 1)
                    pe.wait_ge(attnT_copied, after(row, G, g + 1))
                    pe.matmul(bank[5][:], w1_w[:], attnT[:], start=True, stop=True).then_inc(hid_ready, 1)
                    pe.wait_ge(gelu_ready, after(row, G, g + 1))
                    pe.wait_ge(residual_done, after(row, STAGES, g))
                    for t in range(T):
                        mm = pe.matmul(bank[4][:, P * t:P * (t + 1)], hidT[:, P * t:P * (t + 1)], w2_w[:],
                                       start=True, stop=True)
                    mm.then_inc(mlp_ready, 1)

                def experts(f, k):
                    turn(k)
                    pe.wait_ge(zT_copied, after(row, STAGES, k + 1))
                    pe.wait_ge(zlo_ready, after(row, MOE, f + 1))
                    for t in range(T):
                        cols = slice(P * t, P * (t + 1))
                        for a, b, first, last in ((z_hi, router_hi, True, False), (z_hi, router_lo, False, False),
                                                  (z_lo, router_hi, False, True)):
                            mm = pe.matmul(bank[7][:, NE * t:NE * (t + 1)], a[:, cols], b[:], start=first, stop=last)
                    mm.then_inc(logits_ready, 1)
                    for s in range(CH + 2):
                        if s < CH:
                            n = f * CH + s
                            cols = slice(P * s, P * (s + 1))
                            for hi, lo, b, freed, ready in ((gate_hi, gate_lo, 0, silu_ready, gate_ready),
                                                            (up_hi, up_lo, 2, gated_ready, up_ready)):
                                pe.wait_ge(freed, after(row, MOE * CH, n - 1))
                                dst = bank[b + s % 2][:]
                                pe.matmul(dst, hi[:, cols], z_hi[:], start=True, stop=False)
                                pe.matmul(dst, hi[:, cols], z_lo[:], start=False, stop=False)
                                pe.matmul(dst, lo[:, cols], z_hi[:], start=False, stop=True).then_inc(ready, 1)
                        if s == 1:
                            pe.wait_ge(comb_ready, after(row, MOE, f + 1))
                            for t in range(T):
                                mm = pe.transpose(bank[7][0:3 * NE, P // 2 * t:P // 2 * (t + 1)].bitcast(BF16),
                                                  comb_parts[:, t].rearrange("p a e -> p (a e)"), ident_bf[:])
                            mm.then_inc(combT_ready, 1)
                        if 1 <= s <= CH:
                            n = f * CH + s - 1
                            if s == 1:
                                pe.wait_ge(combT_copied, after(row, MOE, f + 1))
                            pe.wait_ge(hid_gated, after(row, MOE * CH, n - 1))
                            pe.matmul(bank[4 + (s - 1) % 2][:],
                                      expert_sel[:, 2 * (s - 1):2 * s].rearrange("p e n -> p (e n)"), combT[:],
                                      start=True, stop=True).then_inc(spread_ready, 1)
                        if s >= 2:
                            c = s - 2
                            pe.wait_ge(hid_gated, after(row, MOE * CH, f * CH + c + 1))
                            if c == 0:
                                pe.wait_ge(y_copied, after(row, MOE, f))
                            pe.matmul(bank[6], down_w[:, c], hid[:, c % 2], start=(c == 0),
                                      stop=(c == CH - 1)).then_inc(down_done, 1)
                    pe.wait_ge(y_copied, after(row, MOE, f + 1))
                    for t in range(T):
                        mm = pe.transpose(bank[7][:, P * t:P * (t + 1)], yT[:, P * t:P * (t + 1)], ident[:])
                    mm.then_inc(y_turned, 1)

                for g in range(G):
                    experts(g, G + g)

                for g in range(G):
                    k = 2 * G + g
                    turn(k)
                    pe.wait_ge(zT_copied, after(row, STAGES, k + 1))
                    new = seqT[:, WIN + GT * g:WIN + GT * (g + 1)]
                    pe.matmul(bank[6], qkv_b_w[:, 0:D], new, start=True, stop=True).then_inc(q_ready, 1)
                    pe.matmul(bank[7], qkv_b_w[:, D:2 * D], new, start=True, stop=True).then_inc(k_ready, 1)
                    pe.wait_ge(k_copied, after(row, G, g + 1))
                    pe.wait_ge(q_masked, after(row, G, g + 1))

                    def mix(i):
                        pe.wait_ge(probs_normed, after(row, TILES, i + 1))
                        for b in range(NB):
                            copied = probsT_by_act if b % 2 == 0 else probsT_by_dve
                            pe.wait_ge(copied, after(row, TILES * NB // 2, i * NB // 2 + b // 2))
                            for hg in range(HG):
                                mm = pe.transpose(bank[4 + b % 2][0:KW, P * hg:P * (hg + 1)],
                                                  probs[:, i % 2, hg * NB + b], ident[:])
                            mm.then_inc(probsT_ready, 1)
                        if i % T:
                            pe.wait_ge(mix_picked, after(row, TILES, i))
                        for b in range(NB):
                            copied = probsT_by_act if b % 2 == 0 else probsT_by_dve
                            pe.wait_ge(copied, after(row, TILES * NB // 2, i * NB // 2 + b // 2 + 1))
                            for hg in range(HG):
                                feats = slice(QB * hg, QB * (hg + 1))
                                mm = pe.matmul(bank[6][feats, P * b:P * (b + 1)],
                                               vals[:, i % 2, D * b + QB * hg:D * b + QB * (hg + 1)],
                                               probsT[:, b, P * hg:P * (hg + 1)], start=True, stop=True,
                                               tile_position=(0, QB * hg))
                        mm.then_inc(mix_ready, 1)

                    for t in range(T):
                        i = T * g + t
                        if t:
                            pe.wait_ge(v_copied, after(row, TILES, i))
                        for b in range(NB):
                            first = P * i + QB * b
                            mm = pe.matmul(bank[7][0:KW, D * b:D * (b + 1)], seqT[:, first:first + KW],
                                           qkv_b_w[:, 2 * D:], start=True, stop=True)
                        mm.then_inc(v_ready, 1)
                        pe.wait_ge(probs_ready, after(row, TILES, i))
                        for hg in range(HG):
                            pe.matmul(bank[hg][:, 0:NB * KW], ident_bf[:],
                                      window[:, min(i, 1)].rearrange("p b k -> p (b k)"), start=True, stop=False,
                                      skip_group_check=True)
                        for hg in range(HG):
                            feats = slice(QB * hg, QB * (hg + 1))
                            for b in range(NB):
                                first = P * i + QB * b
                                mm = pe.matmul(bank[hg][:, KW * b:KW * (b + 1)],
                                               qm[feats, NB * t + b].rearrange("p j q -> p (j q)"),
                                               keysT[feats, first:first + KW], start=False, stop=(b == NB - 1),
                                               tile_position=(QB * hg, 0), skip_group_check=True)
                        mm.then_inc(scores_ready, 1)
                        if t:
                            mix(i - 1)
                    mix(T * g + T - 1)
                    pe.wait_ge(v_copied, after(row, TILES, T * g + T))
                    pe.wait_ge(mix_picked, after(row, TILES, T * g + T))
                    pe.matmul(bank[7].rearrange("p (t d) -> p t d", d=D), ones_row[:],
                              bout_row[:].unsqueeze(1).broadcast_to([1, T, D]), start=True, stop=False,
                              skip_group_check=True)
                    for t in range(T):
                        mm = pe.matmul(bank[7][:, P * t:P * (t + 1)], mixT[:, t], out_w[:], start=False,
                                       stop=(t == T - 1), skip_group_check=True)
                    mm.then_inc(proj_ready, 1)

                for g in range(G):
                    experts(G + g, 3 * G + g)


_NAMES = ("x", "wqkv_a", "lam", "g1", "g2", "g3", "w1", "w2", "wqkv_b", "wout", "bout", "wgate", "wg", "wu", "wd")


def kernel(L0_attn_a_x, L0_attn_a_Wq, L0_attn_a_Wk, L0_attn_a_Wv, L0_attn_a_lambda_params, L0_attn_a_g1,
           L0_attn_a_g2, L0_attn_a_g3, L0_attn_a_W1, L0_attn_a_W2, L0_attn_b_w_qkv, L0_attn_b_w_out,
           L0_attn_b_b_out, L0_ffn_gate_w, L0_ffn_gate_up_w, L0_ffn_down_w):
    import concourse.bacc as bacc
    from concourse.bass_utils import run_bass_kernel_spmd

    gate_up = np.transpose(np.asarray(L0_ffn_gate_up_w), (2, 0, 1))
    arrays = (
        np.reshape(np.asarray(L0_attn_a_x), (ROWS * SEQ, D)),
        np.transpose(np.concatenate([np.asarray(a) for a in (L0_attn_a_Wq, L0_attn_a_Wk, L0_attn_a_Wv)])),
        L0_attn_a_lambda_params, L0_attn_a_g1, L0_attn_a_g2, L0_attn_a_g3,
        np.transpose(np.asarray(L0_attn_a_W1)), np.transpose(np.asarray(L0_attn_a_W2)),
        np.transpose(np.asarray(L0_attn_b_w_qkv)), np.transpose(np.asarray(L0_attn_b_w_out)), L0_attn_b_b_out,
        np.transpose(np.asarray(L0_ffn_gate_w)),
        np.reshape(gate_up[:, :, 0:ED], (D, NE * ED)), np.reshape(gate_up[:, :, ED:], (D, NE * ED)),
        np.reshape(np.transpose(np.asarray(L0_ffn_down_w), (0, 2, 1)), (NE * ED, D)),
    )
    nc = bacc.Bacc("TRN2", target_bir_lowering=False, num_devices=1)
    feeds, args = {}, []
    for name, a in zip(_NAMES, arrays):
        a = np.ascontiguousarray(a)
        feeds[name] = a
        args.append(nc.dram_tensor(name, a.shape, mybir.dt.from_np(a.dtype), kind="ExternalInput").ap())
    args.append(nc.dram_tensor("out", (ROWS * SEQ, D), F32, kind="ExternalOutput").ap())
    hybrid_block(nc, *args)
    ran = run_bass_kernel_spmd(nc, [feeds], core_ids=[0])
    return np.reshape(ran.results[0]["out"], (ROWS, SEQ, D))
```

```python
from contextlib import ExitStack

import numpy as np

import concourse.bass as bass
from concourse import mybir

F32 = mybir.dt.float32
F32R = mybir.dt.float32r
BF16 = mybir.dt.bfloat16
I32 = mybir.dt.int32
ALU = mybir.AluOpType
ACT = mybir.ActivationFunctionType
AX_X = mybir.AxisListType.X

P = 128
ROWS, SEQ, D = 4, 1024, 128
T = 4
GT = T * P
G = SEQ // GT
TILES = SEQ // P
H, HD = 16, 8
HALF = HD // 2
NE, ED = 32, 64
TOP = 8
CH = NE * ED // P
MOE = 2 * G
QB = 32
WIN = 64
KW = WIN + QB
HG = P // QB
NB = P // QB
NEG = -3.0e38
LN_EPS = 1e-5
RMS_EPS = float(np.finfo(np.float32).eps)
LAMBDA_INIT = 0.8 - 0.6 * float(np.exp(-0.3 * 0))
KV_SCALE = 1.0 / float(np.sqrt(D // 2))
Q_SCALE = 1.0 / float(np.sqrt(HD))
RSQRT_MAGIC = float(0x5F3759DF)
VECTOR_STEPS = 296
VECTOR_STEPS_AHEAD = 169

IN_BANK7 = {"x_turn", "qkv", "attnT", "mlp1", "mlp2", "moe_turn", "route", "weighT", "y_back",
            "seq_turn", "keys", "queries", "vals", "proj"}
Z_USERS = {"x_norm", "moe_norm", "seq_norm"}
TURNS = {"x_turn", "moe_turn", "seq_turn"}


def ahead(*steps):
    return [(name, n, 1) for name, n in steps]


def own(*steps):
    return [(name, n, 0) for name, n in steps]


PLAN = {
    ("moe", 0): {1: own(("moe_norm", 1)), 3: own(("moe_turn", 1), ("route", 1)), 5: own(("weigh", 1)),
                 7: own(("weighT", 1)), 8: ahead(("x_norm", 0)), 10: ahead(("x_turn", 0)),
                 11: ahead(("qkv", 0), ("qkv", 1)), 13: ahead(("attend", 0)), 15: ahead(("attend", 1))},
    ("moe", 1): {0: own(("y_back", 0)), 1: own(("seq_norm", 0)), 3: own(("seq_turn", 0)), 4: own(("keys", 0)),
                 5: own(("queries", 0)), 6: ahead(("qkv", 2), ("qkv", 3)), 7: ahead(("attend", 2)),
                 9: ahead(("attend", 3)), 11: ahead(("heads", 0)), 13: ahead(("attnT", 0)),
                 14: ahead(("mlp1", 0)), 15: ahead(("mlp2", 0))},
    ("attn", 0): {0: own(("vals", 0), ("y_back", 1)), 1: own(("vals", 1), ("seq_norm", 1)),
                  2: own(("vals", 2), ("seq_turn", 1), ("keys", 1)), 3: own(("vals", 3), ("queries", 1)),
                  4: own(("vals", 4)), 5: own(("vals", 5), ("proj", 0), ("moe_norm", 2)),
                  6: own(("vals", 6), ("moe_turn", 2), ("route", 2)), 7: own(("vals", 7), ("weigh", 2), ("weighT", 2))},
    ("moe", 2): {0: own(("proj", 1)), 1: own(("moe_norm", 3)), 3: own(("moe_turn", 3), ("route", 3)),
                 5: own(("weigh", 3)), 7: own(("weighT", 3)), 8: ahead(("x_norm", 1)), 10: ahead(("x_turn", 1)),
                 11: ahead(("qkv", 4), ("qkv", 5)), 13: ahead(("attend", 4)), 15: ahead(("attend", 5))},
    ("moe", 3): {0: own(("y_back", 2)), 1: ahead(("moe_norm", 0)), 3: ahead(("moe_turn", 0), ("route", 0)),
                 4: ahead(("weigh", 0)), 5: ahead(("weighT", 0)), 6: ahead(("qkv", 6), ("qkv", 7)),
                 7: ahead(("attend", 6)), 9: ahead(("attend", 7)), 11: ahead(("heads", 1)), 13: ahead(("attnT", 1)),
                 14: ahead(("mlp1", 1)), 15: ahead(("mlp2", 1)), 17: own(("y_back", 3))},
}
AHEAD = [(name, n, 0) for name, n in (
    ("x_norm", 0), ("x_turn", 0), ("qkv", 0), ("qkv", 1), ("attend", 0), ("qkv", 2), ("attend", 1), ("qkv", 3),
    ("x_norm", 1), ("x_turn", 1), ("attend", 2), ("qkv", 4), ("attend", 3), ("qkv", 5), ("heads", 0), ("attnT", 0),
    ("mlp1", 0), ("mlp2", 0), ("attend", 4), ("qkv", 6), ("attend", 5), ("qkv", 7), ("moe_norm", 0), ("moe_turn", 0),
    ("route", 0), ("weigh", 0), ("weighT", 0), ("attend", 6), ("attend", 7), ("heads", 1), ("attnT", 1), ("mlp1", 1),
    ("mlp2", 1))]


def count(steps, names):
    return sum(name in names for name, _, _ in steps)


ROW_STEPS = [step for slots in PLAN.values() for at in sorted(slots) for step in slots[at]]


class Walk:

    def __init__(self, row, in_front, last=False):
        self.row, self.last = row, last
        self.first = 0 if in_front else count(AHEAD, IN_BANK7) + row * count(ROW_STEPS, IN_BANK7)
        self.first_z = 0 if in_front else count(AHEAD, Z_USERS) + row * count(ROW_STEPS, Z_USERS)
        self.products = self.norms = 0
        self.passed = {}

    def after_step(self, name, n):
        return self.first + self.passed.get((name, n), 0) + 1

    def after_last(self, names):
        return self.first + max([at for (name, _), at in self.passed.items() if name in names], default=0) + 1

    def after_norms(self):
        return self.first_z + self.norms + 1

    def steps(self, steps, engine_steps):
        for name, n, rows in steps:
            if rows and self.last:
                continue
            if name in engine_steps:
                engine_steps[name](self.row + rows, n, self.first + self.products + 1, self)
            self.products += name in IN_BANK7
            self.norms += name in Z_USERS
            if name in IN_BANK7:
                self.passed[name, n] = self.products

    def slot(self, stage, at, engine_steps):
        self.steps(PLAN[stage].get(at, []), engine_steps)


def hybrid_block(nc, x, wqkv_a, lam, g1, g2, g3, w1, w2, wqkv_b, wout, bout, wgate, wg, wu, wd, out):
    x_rows = x.rearrange("(r t p) d -> r p t d", r=ROWS, p=P)
    out_rows = out.rearrange("(r t p) d -> r p t d", r=ROWS, p=P)

    with ExitStack() as ctx:
        def sb(name, shape, dt=F32):
            return ctx.enter_context(nc.sbuf_tensor(name, shape, dt))

        def sem(name):
            return ctx.enter_context(nc.semaphore(name))

        qkv_a_w = sb("qkv_a_w", [P, 3 * D])
        w1_w, w2_w = sb("w1_w", [P, D]), sb("w2_w", [P, D])
        qkv_b_w, out_w = sb("qkv_b_w", [P, 3 * D]), sb("out_w", [P, D])
        bout_row = sb("bout_row", [1, D])
        router_w = sb("router_w", [P, NE])
        stage_w = sb("stage_w", [P, NE * ED])
        gate_hi, gate_lo = sb("gate_hi", [P, NE * ED], F32R), sb("gate_lo", [P, NE * ED], F32R)
        up_hi, up_lo = sb("up_hi", [P, NE * ED], F32R), sb("up_lo", [P, NE * ED], F32R)
        router_hi, router_lo = sb("router_hi", [P, NE], F32R), sb("router_lo", [P, NE], F32R)
        down_w = sb("down_w", [P, CH, D])
        g1_col, g2_row, g3_row = sb("g1_col", [P, 1]), sb("g2_row", [P, HD]), sb("g3_row", [P, D])
        lam_row, lam_prod, lam_exp = sb("lam_row", [P, 4]), sb("lam_prod", [P, 2]), sb("lam_exp", [P, 2])
        lam_diff = sb("lam_diff", [P, 1])
        kv_coef = sb("kv_coef", [P, HD * HD])
        ident, ident_bf = sb("ident", [P, P]), sb("ident_bf", [P, P], BF16)
        ones_row = sb("ones_row", [1, P])
        head_bits, head_mask = sb("head_bits", [P, HG, HG]), sb("head_mask", [P, HG])
        q_mask = sb("q_mask", [P, HG])
        window = sb("window", [P, 2, NB, KW], BF16)
        expert_sel = sb("expert_sel", [3 * NE, NE, ED], BF16)

        x_in, x_mid, xs, x_out = (sb(n, [P, TILES, D]) for n in ("x_in", "x_mid", "xs", "x_out"))
        stats, moments = sb("stats", [P, T, 6]), sb("moments", [P, T, 2])
        rstd, msq, rms = sb("rstd", [P, T]), sb("msq", [P, T]), sb("rms", [P, T])
        z = sb("z", [P, T, D])
        zT = sb("zT", [P, GT])
        qkv = sb("qkv", [P, 2, 3 * D])
        eneg = sb("eneg", [P, 2, 2 * D])
        elu = sb("elu", [P, 2, 2 * D])
        kv_terms, w_terms = sb("kv_terms", [P, 2, HD * HD * H]), sb("w_terms", [P, H * HD * HD])
        kv = sb("kv", [P, HD * HD])
        attn, squares = sb("attn", [P, T, D]), sb("squares", [P, T, D])
        head_rms, tok_rms = sb("head_rms", [P, T * H]), sb("tok_rms", [P, T])
        wait_carrier, taken_mark = sb("wait_carrier", [P, 1]), sb("taken_mark", [P, 1])
        var_eps, newton = sb("var_eps", [P, T]), sb("newton", [P, T * H])
        head_ms, tok_ms = sb("head_ms", [P, T * H]), sb("tok_ms", [P, T])
        gain = sb("gain", [P, T, D])
        attn_sum = sb("attn_sum", [P, T, D])
        attnT, hidT = sb("attnT", [P, GT]), sb("hidT", [P, GT])
        z_hi, z_lo = sb("z_hi", [P, 2, GT], F32R), sb("z_lo", [P, 2, GT], F32R)
        logits, top, shifted = sb("logits", [P, T, NE]), sb("top", [P, T, TOP]), sb("shifted", [P, T, NE])
        expd, top_exp, replaced = sb("expd", [P, T, NE]), sb("top_exp", [P, T, TOP]), sb("replaced", [P, T, NE])
        top_sum, top_inv = sb("top_sum", [P, T]), sb("top_inv", [P, T])
        comb, comb_rest = sb("comb", [P, T, NE]), sb("comb_rest", [P, 2, T, NE])
        comb_parts = sb("comb_parts", [P, T, 3, NE], BF16)
        combT = sb("combT", [3 * NE, 2, GT], BF16)
        silu, gated, hid = (sb(n, [P, 2, GT]) for n in ("silu", "gated", "hid"))
        yT = sb("yT", [P, GT])
        seqT, keysT = sb("seqT", [P, WIN + SEQ]), sb("keysT", [P, WIN + SEQ])
        qm = sb("qm", [P, NB * T, HG, QB])
        vals = sb("vals", [KW, 2, NB * D])
        neg_max, prob_sum, prob_inv = (sb(n, [P, 2, NB * HG]) for n in ("neg_max", "prob_sum", "prob_inv"))
        probs = sb("probs", [P, 2, NB * HG, KW])
        probsT = sb("probsT", [KW, NB, HG * P])
        mixT = sb("mixT", [P, TILES, P])
        mix_part = sb("mix_part", [P, 3, P])

        bank = [ctx.enter_context(nc.psum_tensor(f"bank{i}", [P, 512], F32))[:] for i in range(8)]
        side = bank[7]

        weights_in, x_loaded, x_stored = sem("weights_in"), sem("x_loaded"), sem("x_stored")
        pool_const, const_ready, setup_step = sem("pool_const"), sem("const_ready"), sem("setup_step")
        vector_step = sem("vector_step")
        side_ready, side_taken = sem("side_ready"), sem("side_taken")
        z_ready = sem("z_ready")
        eneg_ready, elu_ready = sem("eneg_ready"), sem("elu_ready")
        kv_terms_ready, kv_summed = sem("kv_terms_ready"), sem("kv_summed")
        attn_ready, attn_added, attn_a_done = sem("attn_ready"), sem("attn_added"), sem("attn_a_done")
        zhi_ready, shifted_ready, expd_ready = sem("zhi_ready"), sem("shifted_ready"), sem("expd_ready")
        comb_ready = sem("comb_ready")
        gate_ready, up_ready, spread_ready = sem("gate_ready"), sem("up_ready"), sem("spread_ready")
        silu_ready, gated_ready, hid_gated = sem("silu_ready"), sem("gated_ready"), sem("hid_gated")
        down_done, y_copied, moe_done = sem("down_done"), sem("y_copied"), sem("moe_done")
        scores_ready, max_ready, probs_ready = sem("scores_ready"), sem("max_ready"), sem("probs_ready")
        inv_ready, probs_normed = sem("inv_ready"), sem("probs_normed")
        probsT_ready, probsT_copied = sem("probsT_ready"), sem("probsT_copied")
        mix_ready, mix_picked, attn_b_done = sem("mix_ready"), sem("mix_picked"), sem("attn_b_done")
        loop_sems = (x_loaded, x_stored, side_ready, side_taken, z_ready, eneg_ready, elu_ready,
                     kv_terms_ready, kv_summed, attn_ready, attn_added, attn_a_done, zhi_ready, shifted_ready,
                     expd_ready, comb_ready, gate_ready, up_ready, spread_ready, silu_ready,
                     gated_ready, hid_gated, down_done, y_copied, moe_done,
                     scores_ready, max_ready, probs_ready, inv_ready, probs_normed, probsT_ready,
                     probsT_copied, mix_ready, mix_picked, attn_b_done)

        loads = [(qkv_a_w[:], wqkv_a), (w1_w[:], w1), (w2_w[:], w2), (qkv_b_w[:], wqkv_b), (out_w[:], wout),
                 (bout_row[:], bout.rearrange("(a n) -> a n", a=1)), (router_w[:], wgate),
                 (down_w[:], wd.rearrange("(c p) d -> p c d", p=P)),
                 (g1_col[:], g1.rearrange("(p a) -> p a", a=1)), (g2_row[:], g2.partition_broadcast(P)),
                 (g3_row[:], g3.partition_broadcast(P)), (lam_row[:], lam.partition_broadcast(P))]
        N_LOADS = len(loads)

        def after(row, per_row, n):
            return row * per_row + max(n, 0) + 1

        def rows_of(engine, run):
            with engine.Fori(0, ROWS - 1) as row:
                run(row, Walk(row, False))
            run(ROWS - 1, Walk(ROWS - 1, False, last=True))

        block = ctx.enter_context(nc.Block())

        @block.sync
        def _(sp):
            for started in loop_sems:
                sp.sem_inc(started, 1)
            sp.dma_start(x_in[:], x_rows[0]).then_inc(x_loaded, 16)
            for dst, src in loads:
                sp.dma_start(dst, src).then_inc(weights_in, 16)
            sp.dma_start(stage_w[:], wg).then_inc(weights_in, 16)
            sp.wait_ge(const_ready, 2)
            sp.dma_start(stage_w[:], wu).then_inc(weights_in, 16)
            with sp.Fori(0, ROWS - 1) as row:
                sp.wait_ge(attn_added, after(row, G, G))
                sp.dma_start(x_in[:], x_rows[row + 1]).then_inc(x_loaded, 16)
                sp.wait_ge(moe_done, after(row, MOE, MOE))
                sp.dma_start(out_rows[row], x_out[:]).then_inc(x_stored, 16)
            sp.wait_ge(moe_done, after(ROWS - 1, MOE, MOE))
            sp.dma_start(out_rows[ROWS - 1], x_out[:]).then_inc(x_stored, 16)
            sp.wait_ge(x_stored, after(ROWS, 16, 0))

        @block.gpsimd
        def _(pool):
            n = [0]

            def step(ins):
                n[0] += 1
                ins.then_inc(pool_const, 1)
                pool.wait_ge(pool_const, n[0])

            step(pool.memset(ident[:], 0.0))
            step(pool.memset(ident_bf[:], 0.0))
            for t in (ident, ident_bf):
                step(pool.affine_select(out=t[:], in_=t[:], compare_op=ALU.not_equal, fill=1.0, base=0,
                                        pattern=[[-1, P]], channel_multiplier=1))
            step(pool.memset(ones_row[:], 1.0))
            step(pool.memset(head_bits[:], 1.0))
            step(pool.affine_select(out=head_bits[:], in_=head_bits[:], compare_op=ALU.is_ge, fill=0.0, base=0,
                                    pattern=[[-HG * HD, HG], [-HD, HG]], channel_multiplier=1))
            step(pool.affine_select(out=head_bits[:], in_=head_bits[:], compare_op=ALU.is_ge, fill=0.0,
                                    base=HD - 1, pattern=[[HG * HD, HG], [HD, HG]], channel_multiplier=-1))
            step(pool.memset(window[:], 0.0))
            for j in range(HG):
                rows = window[QB * j:QB * (j + 1)]
                step(pool.affine_select(out=rows, in_=rows, compare_op=ALU.is_gt, fill=NEG, base=0,
                                        pattern=[[0, 2], [0, NB], [1, KW]], channel_multiplier=-1))
                step(pool.affine_select(out=rows, in_=rows, compare_op=ALU.is_ge, fill=NEG, base=WIN,
                                        pattern=[[0, 2], [0, NB], [-1, KW]], channel_multiplier=1))
            for b in range(WIN // QB):
                step(pool.memset(window[:, 0, b, 0:WIN - QB * b], NEG))
            step(pool.memset(expert_sel[:], 0.0))
            for part in range(3):
                step(pool.affine_select(out=expert_sel[:], in_=expert_sel[:], compare_op=ALU.not_equal,
                                        fill=1.0, base=-NE * part, pattern=[[-1, NE], [0, ED]],
                                        channel_multiplier=1))
            step(pool.memset(seqT[:, 0:WIN], 0.0))
            step(pool.memset(keysT[:, 0:WIN], 0.0))
            pool.memset(kv_coef[:], KV_SCALE).then_inc(const_ready, 1)
            def attend(row, i, product, walk):
                pool.wait_ge(elu_ready, after(row, TILES, i + 1))
                pool.wait_ge(kv_summed, after(row, TILES, i - 1))
                k = elu[:, i % 2, D:2 * D].rearrange("p (h e) -> p e h", e=HD)
                v = qkv[:, i % 2, 2 * D:3 * D].rearrange("p (h d) -> p d h", d=HD)
                pool.tensor_tensor(
                    kv_terms[:, i % 2].rearrange("p (e d h) -> p e d h", e=HD, d=HD),
                    k.unsqueeze(2).broadcast_to([P, HD, HD, H]),
                    v.unsqueeze(1).broadcast_to([P, HD, HD, H]), ALU.mult).then_inc(kv_terms_ready, 1)

            def heads(row, g, product, walk):
                pool.wait_ge(attn_ready, after(row, G, g + 1))
                pool.wait_ge(x_loaded, after(row, 16, 16))
                if not isinstance(row, int):
                    pool.wait_ge(moe_done, after(row - 1, MOE, g + 1))
                pool.tensor_tensor(x_mid[:, T * g:T * g + T], x_in[:, T * g:T * g + T], attn_sum[:],
                                   ALU.add).then_inc(attn_added, 1)

            steps = {"attend": attend, "heads": heads}
            Walk(0, True).steps(AHEAD, steps)

            def run(row, walk):
                for stage, slots in PLAN.items():
                    for at in range(max(slots) + 1):
                        if stage[0] == "attn":
                            pool.wait_ge(inv_ready, after(row, TILES, at + 1))
                            pr = probs[:, at % 2]
                            pool.tensor_tensor(
                                pr, pr, prob_inv[:, at % 2].unsqueeze(2).broadcast_to([P, NB * HG, KW]),
                                ALU.mult).then_inc(probs_normed, 1)
                        walk.slot(stage, at, steps)

            rows_of(pool, run)

        @block.scalar
        def _(act):
            act.wait_ge(weights_in, 16 * N_LOADS)
            act.wait_ge(setup_step, 1)
            act.activation(lam_exp[:], lam_prod[:], ACT.Exp).then_inc(setup_step, 1)

            def copy_side(dst, product, src=side):
                act.wait_ge(side_ready, product + 1)
                act.activation(dst, src, ACT.Copy).then_inc(side_taken, 1)

            def x_turn(row, g, product, walk):
                copy_side(zT[:], product)

            def qkv_step(row, i, product, walk):
                act.wait_ge(side_ready, product + 1)
                act.wait_ge(kv_terms_ready, after(row, TILES, i - 1))
                act.activation(qkv[:, i % 2], side[:, 0:3 * D], ACT.Copy)
                act.activation(eneg[:, i % 2], side[:, 0:2 * D], ACT.Relu, scale=-1.0).then_inc(side_taken, 1)
                act.wait_ge(side_taken, product + 1)
                act.activation(eneg[:, i % 2], eneg[:, i % 2], ACT.Exp, scale=-1.0).then_inc(eneg_ready, 1)

            def attnT_step(row, g, product, walk):
                copy_side(attnT[:], product)

            def mlp1(row, g, product, walk):
                act.wait_ge(side_ready, product + 1)
                act.activation(hidT[:], side, ACT.Gelu).then_inc(side_taken, 1)

            def moe_turn(row, f, product, walk):
                act.wait_ge(side_ready, product + 1)
                act.activation(z_hi[:, f % 2], side, ACT.Copy).then_inc(zhi_ready, 1)

            def weigh(row, f, product, walk):
                act.wait_ge(shifted_ready, after(row, MOE, f + 1))
                act.activation(expd[:], shifted[:], ACT.Exp).then_inc(expd_ready, 1)

            def weighT(row, f, product, walk):
                act.wait_ge(side_ready, product + 1)
                act.activation(combT[:, f % 2], side[0:3 * NE, 0:GT // 2].bitcast(BF16),
                               ACT.Copy).then_inc(side_taken, 1)

            def seq_turn(row, g, product, walk):
                copy_side(seqT[:, WIN + GT * g:WIN + GT * (g + 1)], product)

            def keys(row, g, product, walk):
                copy_side(keysT[:, WIN + GT * g:WIN + GT * (g + 1)], product)

            def queries(row, g, product, walk):
                act.wait_ge(side_ready, product + 1)
                for j in range(HG):
                    a = act.activation(qm[:, :, j, :], side.rearrange("p (b q) -> p b q", q=QB),
                                       ACT.Copy, scale=q_mask[:, j:j + 1])
                a.then_inc(side_taken, 1)

            def vals_step(row, i, product, walk):
                act.wait_ge(side_ready, product + 1)
                act.activation(vals[:, i % 2], side[0:KW, :], ACT.Copy).then_inc(side_taken, 1)

            steps = {"x_turn": x_turn, "qkv": qkv_step, "attnT": attnT_step, "mlp1": mlp1, "moe_turn": moe_turn,
                     "weigh": weigh, "weighT": weighT, "seq_turn": seq_turn, "keys": keys, "queries": queries,
                     "vals": vals_step}
            Walk(0, True).steps(AHEAD, steps)

            def run(row, walk):
                for stage, slots in PLAN.items():
                    kind, f = stage
                    for at in range(CH if kind == "moe" else TILES):
                        if kind == "moe":
                            n = f * CH + at
                            act.wait_ge(gate_ready, after(row, MOE * CH, n + 1))
                            act.wait_ge(gated_ready, after(row, MOE * CH, n - 1))
                            act.activation(silu[:, at % 2], bank[at % 2], ACT.Silu).then_inc(silu_ready, 1)
                        else:
                            act.wait_ge(probsT_ready, after(row, TILES * NB, (at - 1) * NB))
                            act.wait_ge(inv_ready, after(row, TILES, at - 1))
                            for hg in range(HG):
                                act.wait_ge(max_ready, after(row, TILES * HG, at * HG + hg + 1))
                                for b in range(NB):
                                    m = hg * NB + b
                                    a = act.activation(probs[:, at % 2, m], bank[hg][:, b * KW:(b + 1) * KW],
                                                       ACT.Exp, bias=neg_max[:, at % 2, m:m + 1],
                                                       accum_out=prob_sum[:, at % 2, m:m + 1])
                                a.then_inc(probs_ready, 1)
                        walk.slot(stage, at, steps)
                    if kind == "moe":
                        act.wait_ge(down_done, after(row, MOE * CH, f * CH + CH))
                        act.activation(yT[:], bank[6], ACT.Copy).then_inc(y_copied, 1)

            rows_of(act, run)

        @block.vector
        def _(dve):
            dve.wait_ge(weights_in, 16 * (N_LOADS + 1))
            dve.wait_ge(pool_const, 1)
            dve.tensor_scalar(qkv_a_w[:], qkv_a_w[:], g1_col[:, 0:1], None, ALU.mult)
            dve.tensor_copy(gate_hi[:], stage_w[:])
            dve.tensor_copy(router_hi[:], router_w[:])
            dve.tensor_tensor(lam_prod[:], lam_row[:, 0:4:2], lam_row[:, 1:4:2], ALU.mult).then_inc(setup_step, 1)
            dve.wait_ge(setup_step, 2)
            dve.tensor_tensor(gate_lo[:], stage_w[:], gate_hi[:], ALU.subtract).then_inc(const_ready, 1)
            dve.tensor_tensor(router_lo[:], router_w[:], router_hi[:], ALU.subtract)
            dve.wait_ge(weights_in, 16 * (N_LOADS + 2))
            dve.tensor_copy(up_hi[:], stage_w[:]).then_inc(setup_step, 1)
            dve.wait_ge(setup_step, 3)
            dve.tensor_tensor(up_lo[:], stage_w[:], up_hi[:], ALU.subtract).then_inc(setup_step, 1)
            dve.tensor_tensor(lam_diff[:], lam_exp[:, 0:1], lam_exp[:, 1:2], ALU.subtract).then_inc(setup_step, 1)
            dve.wait_ge(setup_step, 5)
            dve.tensor_scalar(lam_diff[:], lam_diff[:], LAMBDA_INIT, -1.0, ALU.add, ALU.mult).then_inc(setup_step, 1)
            dve.wait_ge(setup_step, 6)
            dve.wait_ge(const_ready, 2)
            dve.tensor_scalar(kv_coef[:, HALF * HD:], kv_coef[:, HALF * HD:], lam_diff[:, 0:1], None, ALU.mult)
            dve.tensor_scalar(g2_row[:], g2_row[:], 1.0 - LAMBDA_INIT, None, ALU.mult)
            dve.tensor_reduce(head_mask[:], head_bits[:].rearrange("p g j -> p j g"), AX_X, ALU.add).then_inc(setup_step, 1)
            dve.wait_ge(setup_step, 7)
            dve.tensor_scalar(q_mask[:], head_mask[:], Q_SCALE, None, ALU.mult).then_inc(const_ready, 1)
            dve.wait_ge(const_ready, 3)
            marks, first_mark = [0], [0]

            def mark(ins):
                marks[0] += 1
                ins.then_inc(vector_step, 1)

            def settle():
                dve.wait_ge(vector_step, first_mark[0] + marks[0])

            def step(ins):
                mark(ins)
                settle()

            def carry():
                dve.memset(wait_carrier[:], 0.0)

            def inv_sqrt(y, v, tmp):
                step(dve.tensor_single_scalar(tmp.bitcast(I32), v.bitcast(I32), 1, ALU.arith_shift_right))
                step(dve.tensor_scalar(y.bitcast(I32), tmp.bitcast(I32), -1.0, RSQRT_MAGIC, ALU.mult, ALU.add))
                for _ in range(3):
                    step(dve.tensor_tensor(tmp, y, y, ALU.mult))
                    step(dve.scalar_tensor_tensor(out=tmp, in0=tmp, scalar=-0.5, in1=v, op0=ALU.mult,
                                                  op1=ALU.mult))
                    step(dve.scalar_tensor_tensor(out=y, in0=tmp, scalar=1.5, in1=y, op0=ALU.add,
                                                  op1=ALU.mult))

            def norm_group(src, g, walk, with_rms):
                for t in range(T):
                    ins = dve.bn_stats(stats[:, t], src[:, T * g + t])
                step(ins)
                carry()
                for t in range(T):
                    ins = dve.bn_aggr(moments[:, t], stats[:, t])
                step(ins)
                step(dve.tensor_scalar(var_eps[:], moments[:, :, 1], LN_EPS, None, ALU.add))
                inv_sqrt(rstd[:], var_eps[:], newton[:, 0:T])
                if with_rms:
                    step(dve.tensor_tensor(msq[:], rstd[:], rstd[:], ALU.mult))
                    step(dve.tensor_tensor(msq[:], msq[:], moments[:, :, 1], ALU.mult))
                    step(dve.tensor_scalar(msq[:], msq[:], RMS_EPS, None, ALU.add))
                    inv_sqrt(rms[:], msq[:], newton[:, 0:T])
                    step(dve.tensor_tensor(rstd[:], rstd[:], rms[:], ALU.mult))
                dve.wait_ge(side_ready, walk.after_last(TURNS))
                for t in range(T):
                    ins = dve.tensor_scalar(z[:, t], src[:, T * g + t], moments[:, t, 0:1], rstd[:, t:t + 1],
                                            ALU.subtract, ALU.mult)
                ins.then_inc(z_ready, 1)

            def x_norm(row, g, product, walk):
                dve.wait_ge(x_loaded, after(row, 16, 16))
                norm_group(x_in, g, walk, True)

            def moe_norm(row, f, product, walk):
                if f < G:
                    dve.wait_ge(attn_a_done, after(row, G, f + 1))
                else:
                    dve.wait_ge(attn_b_done, after(row, G, f - G + 1))
                norm_group(x_mid if f < G else xs, f % G, walk, False)

            def seq_norm(row, g, product, walk):
                dve.wait_ge(moe_done, after(row, MOE, g + 1))
                norm_group(xs, g, walk, False)

            def qkv_step(row, i, product, walk):
                settle()
                dve.wait_ge(eneg_ready, after(row, TILES, i + 1))
                dve.wait_ge(kv_terms_ready, after(row, TILES, i - 1))
                dve.scalar_tensor_tensor(out=elu[:, i % 2], in0=eneg[:, i % 2], scalar=-1.0,
                                         in1=qkv[:, i % 2, 0:2 * D], op0=ALU.add, op1=ALU.max)\
                   .then_inc(elu_ready, 1)

            def attend(row, i, product, walk):
                dve.wait_ge(kv_terms_ready, after(row, TILES, i + 1))
                dve.tensor_reduce(kv[:], kv_terms[:, i % 2].rearrange("p (c h) -> p c h", h=H), AX_X,
                                  ALU.add).then_inc(kv_summed, 1)
                dve.wait_ge(kv_summed, after(row, TILES, i + 1))
                step(dve.tensor_tensor(kv[:], kv[:], kv_coef[:], ALU.mult))
                q = elu[:, i % 2, 0:D].rearrange("p (h e) -> p h e", e=HD)
                kvT = kv[:].rearrange("p (e d) -> p d e", d=HD)
                step(dve.tensor_tensor(w_terms[:].rearrange("p (h d e) -> p h d e", h=H, d=HD),
                                       q.unsqueeze(2).broadcast_to([P, H, HD, HD]),
                                       kvT.unsqueeze(1).broadcast_to([P, H, HD, HD]), ALU.mult))
                mark(dve.tensor_reduce(attn[:, i % T], w_terms[:].rearrange("p (c e) -> p c e", e=HD), AX_X,
                                       ALU.add))

            def heads(row, g, product, walk):
                settle()
                flat = "p t (h d) -> p (t h) d"
                a3 = attn[:].rearrange(flat, d=HD)
                step(dve.tensor_tensor(squares[:], attn[:], attn[:], ALU.mult))
                step(dve.tensor_reduce(head_ms[:], squares[:].rearrange(flat, d=HD), AX_X, ALU.add))
                step(dve.tensor_scalar(head_ms[:], head_ms[:], 1.0 / HD, RMS_EPS, ALU.mult, ALU.add))
                inv_sqrt(head_rms[:], head_ms[:], newton[:])
                step(dve.tensor_tensor(a3, a3, head_rms[:].unsqueeze(2).broadcast_to([P, T * H, HD]), ALU.mult))
                step(dve.tensor_tensor(a3, a3, g2_row[:].unsqueeze(1).broadcast_to([P, T * H, HD]), ALU.mult))
                step(dve.tensor_tensor(squares[:], attn[:], attn[:], ALU.mult))
                step(dve.tensor_reduce(tok_ms[:], squares[:], AX_X, ALU.add))
                step(dve.tensor_scalar(tok_ms[:], tok_ms[:], 1.0 / D, RMS_EPS, ALU.mult, ALU.add))
                inv_sqrt(tok_rms[:], tok_ms[:], newton[:, 0:T])
                for t in range(T):
                    ins = dve.tensor_scalar(gain[:, t], g3_row[:], tok_rms[:, t:t + 1], 1.0, ALU.mult, ALU.add)
                step(ins)
                dve.wait_ge(attn_a_done, after(row, G, g))
                dve.tensor_tensor(attn_sum[:], attn[:], gain[:], ALU.mult).then_inc(attn_ready, 1)

            def add_side(dst, src, g, product, done):
                dve.wait_ge(side_ready, product + 1)
                flat = "p t d -> p (t d)"
                dve.tensor_tensor(dst[:, T * g:T * g + T].rearrange(flat), src[:, T * g:T * g + T].rearrange(flat),
                                  side, ALU.add).then_inc(done, 1)
                dve.memset(taken_mark[:], 0.0).then_inc(side_taken, 1)

            def mlp2(row, g, product, walk):
                dve.wait_ge(attn_added, after(row, G, g + 1))
                add_side(x_mid, x_mid, g, product, attn_a_done)

            def moe_turn(row, f, product, walk):
                dve.wait_ge(zhi_ready, after(row, MOE, f + 1))
                dve.wait_ge(side_ready, product + 1)
                dve.tensor_tensor(z_lo[:, f % 2], side, z_hi[:, f % 2], ALU.subtract).then_inc(side_taken, 1)

            def route(row, f, product, walk):
                dve.wait_ge(side_ready, product + 1)
                dve.tensor_copy(logits[:].rearrange("p t e -> p (t e)"), side[:, 0:T * NE]).then_inc(side_taken, 1)
                dve.wait_ge(side_taken, product + 1)
                carry()
                for t in range(T):
                    ins = dve.max(top[:, t], logits[:, t])
                step(ins)
                dve.tensor_tensor(shifted[:], logits[:], top[:, :, 0:1].broadcast_to([P, T, NE]),
                                  ALU.subtract).then_inc(shifted_ready, 1)

            def weigh(row, f, product, walk):
                dve.wait_ge(expd_ready, after(row, MOE, f + 1))
                carry()
                for t in range(T):
                    ins = dve.max(top_exp[:, t], expd[:, t])
                step(ins)
                carry()
                for t in range(T):
                    ins = dve.match_replace(replaced[:, t], top_exp[:, t], expd[:, t], -1.0)
                mark(ins)
                step(dve.tensor_reduce(top_sum[:], top_exp[:], AX_X, ALU.add))
                mark(dve.reciprocal(top_inv[:], top_sum[:]))
                step(dve.scalar_tensor_tensor(out=comb[:], in0=replaced[:], scalar=0.0, in1=expd[:],
                                              op0=ALU.is_lt, op1=ALU.mult))
                step(dve.tensor_tensor(comb[:], comb[:], top_inv[:].unsqueeze(2).broadcast_to([P, T, NE]),
                                       ALU.mult))
                dve.wait_ge(side_ready, walk.after_last({"weighT"}))
                step(dve.tensor_copy(comb_parts[:, :, 0], comb[:]))
                step(dve.tensor_tensor(comb_rest[:, 0], comb[:], comb_parts[:, :, 0], ALU.subtract))
                step(dve.tensor_copy(comb_parts[:, :, 1], comb_rest[:, 0]))
                step(dve.tensor_tensor(comb_rest[:, 1], comb_rest[:, 0], comb_parts[:, :, 1], ALU.subtract))
                dve.tensor_copy(comb_parts[:, :, 2], comb_rest[:, 1]).then_inc(comb_ready, 1)

            def y_back(row, f, product, walk):
                if f < G:
                    add_side(xs, x_mid, f, product, moe_done)
                else:
                    dve.wait_ge(x_stored, after(row, 16, 0))
                    add_side(x_out, xs, f - G, product, moe_done)

            def proj(row, g, product, walk):
                add_side(xs, xs, g, product, attn_b_done)

            steps = {"x_norm": x_norm, "moe_norm": moe_norm, "seq_norm": seq_norm, "qkv": qkv_step, "attend": attend,
                     "heads": heads, "mlp2": mlp2, "moe_turn": moe_turn, "route": route, "weigh": weigh,
                     "y_back": y_back, "proj": proj}
            Walk(0, True).steps(AHEAD, steps)
            assert marks[0] == VECTOR_STEPS_AHEAD, ("VECTOR_STEPS_AHEAD", marks[0])

            def run(row, walk):
                marks[0], first_mark[0] = 0, VECTOR_STEPS_AHEAD + row * VECTOR_STEPS

                def gate(n):
                    dve.wait_ge(silu_ready, after(row, MOE * CH, n + 1))
                    dve.wait_ge(up_ready, after(row, MOE * CH, n + 1))
                    dve.wait_ge(hid_gated, after(row, MOE * CH, n - 1))
                    dve.tensor_tensor(gated[:, n % 2], silu[:, n % 2], bank[2 + n % 2], ALU.mult)\
                       .then_inc(gated_ready, 1)

                def spread(n):
                    dve.wait_ge(gated_ready, after(row, MOE * CH, n + 1))
                    dve.wait_ge(spread_ready, after(row, MOE * CH, n + 1))
                    dve.wait_ge(down_done, after(row, MOE * CH, n - 1))
                    dve.tensor_tensor(hid[:, n % 2], gated[:, n % 2], bank[4 + n % 2], ALU.mult)\
                       .then_inc(hid_gated, 1)

                def maxima(i):
                    dve.wait_ge(probs_ready, after(row, TILES * HG, (i - 1) * HG))
                    for hg in range(HG):
                        dve.wait_ge(scores_ready, after(row, TILES * HG, i * HG + hg + 1))
                        dve.tensor_reduce(neg_max[:, i % 2, hg * NB:(hg + 1) * NB],
                                          bank[hg][:, 0:NB * KW].rearrange("p (b k) -> p b k", k=KW),
                                          AX_X, ALU.max, negate=True).then_inc(max_ready, 1)

                def finish(i):
                    for b in range(NB):
                        dve.wait_ge(probsT_ready, after(row, TILES * NB, i * NB + b + 1))
                        dve.wait_ge(mix_ready, after(row, TILES, i))
                        dve.tensor_copy(probsT[:, b], bank[4 + b % 2][0:KW, :]).then_inc(probsT_copied, 1)
                    dve.wait_ge(mix_ready, after(row, TILES, i + 1))
                    mix = bank[6].rearrange("p (b j q) -> p j b q", b=NB, j=HG)
                    part = lambda a: a.rearrange("p (b q) -> p b q", q=QB)
                    step(dve.tensor_scalar(part(mix_part[:, 0]), mix[:, 0], head_mask[:, 0:1], None, ALU.mult))
                    for j in range(1, HG):
                        dst = part(mix_part[:, j]) if j < HG - 1 else part(mixT[:, i])
                        ins = dve.scalar_tensor_tensor(out=dst, in0=mix[:, j], scalar=head_mask[:, j:j + 1],
                                                       in1=part(mix_part[:, j - 1]), op0=ALU.mult, op1=ALU.add)
                        if j < HG - 1:
                            step(ins)
                        else:
                            ins.then_inc(mix_picked, 1)

                for stage in PLAN:
                    kind, f = stage
                    if kind == "moe":
                        for s in range(CH + 2):
                            if s < CH:
                                gate(f * CH + s)
                            if 1 <= s <= CH:
                                spread(f * CH + s - 1)
                            walk.slot(stage, s, steps)
                    else:
                        for i in range(TILES):
                            maxima(i)
                            if i:
                                finish(i - 1)
                            dve.wait_ge(probs_ready, after(row, TILES * HG, (i + 1) * HG))
                            dve.wait_ge(probs_normed, after(row, TILES, i - 1))
                            dve.reciprocal(prob_inv[:, i % 2], prob_sum[:, i % 2]).then_inc(inv_ready, 1)
                            walk.slot(stage, i, steps)
                        finish(TILES - 1)
                assert walk.last or marks[0] == VECTOR_STEPS, ("VECTOR_STEPS", marks[0])

            rows_of(dve, run)

        @block.tensor
        def _(pe):
            pe.wait_ge(const_ready, 3)
            pe.wait_ge(setup_step, 7)

            def turn_z(row, n, product, walk):
                pe.wait_ge(z_ready, walk.after_norms())
                pe.wait_ge(side_taken, product)
                for t in range(T):
                    mm = pe.transpose(side[:, P * t:P * (t + 1)], z[:, t], ident[:])
                mm.then_inc(side_ready, 1)

            def qkv_step(row, i, product, walk):
                pe.wait_ge(side_taken, product)
                t = i % T
                pe.matmul(side[:, 0:3 * D], zT[:, P * t:P * (t + 1)], qkv_a_w[:],
                          start=True, stop=True).then_inc(side_ready, 1)

            def attnT_step(row, g, product, walk):
                pe.wait_ge(attn_ready, after(row, G, g + 1))
                pe.wait_ge(side_taken, product)
                for t in range(T):
                    mm = pe.transpose(side[:, P * t:P * (t + 1)], attn_sum[:, t], ident[:])
                mm.then_inc(side_ready, 1)

            def mlp1(row, g, product, walk):
                pe.wait_ge(side_taken, product)
                pe.matmul(side, w1_w[:], attnT[:], start=True, stop=True).then_inc(side_ready, 1)

            def mlp2(row, g, product, walk):
                pe.wait_ge(side_taken, product)
                for t in range(T):
                    mm = pe.matmul(side[:, P * t:P * (t + 1)], hidT[:, P * t:P * (t + 1)], w2_w[:],
                                   start=True, stop=True)
                mm.then_inc(side_ready, 1)

            def route(row, f, product, walk):
                pe.wait_ge(side_taken, product)
                for t in range(T):
                    cols = slice(P * t, P * (t + 1))
                    for a, b, first, last in ((z_hi, router_hi, True, False), (z_hi, router_lo, False, False),
                                              (z_lo, router_hi, False, True)):
                        mm = pe.matmul(side[:, NE * t:NE * (t + 1)], a[:, f % 2, cols], b[:], start=first, stop=last)
                mm.then_inc(side_ready, 1)

            def weighT(row, f, product, walk):
                pe.wait_ge(comb_ready, after(row, MOE, f + 1))
                pe.wait_ge(side_taken, product)
                for t in range(T):
                    mm = pe.transpose(side[0:3 * NE, P // 2 * t:P // 2 * (t + 1)].bitcast(BF16),
                                      comb_parts[:, t].rearrange("p a e -> p (a e)"), ident_bf[:])
                mm.then_inc(side_ready, 1)

            def y_back(row, f, product, walk):
                pe.wait_ge(y_copied, after(row, MOE, f + 1))
                pe.wait_ge(side_taken, product)
                for t in range(T):
                    mm = pe.transpose(side[:, P * t:P * (t + 1)], yT[:, P * t:P * (t + 1)], ident[:])
                mm.then_inc(side_ready, 1)

            def keys(row, g, product, walk):
                pe.wait_ge(side_taken, product)
                pe.matmul(side, qkv_b_w[:, D:2 * D], seqT[:, WIN + GT * g:WIN + GT * (g + 1)],
                          start=True, stop=True).then_inc(side_ready, 1)

            def queries(row, g, product, walk):
                pe.wait_ge(side_taken, product)
                pe.matmul(side, qkv_b_w[:, 0:D], seqT[:, WIN + GT * g:WIN + GT * (g + 1)],
                          start=True, stop=True).then_inc(side_ready, 1)

            def vals_step(row, i, product, walk):
                pe.wait_ge(side_taken, product)
                for b in range(NB):
                    first = P * i + QB * b
                    mm = pe.matmul(side[0:KW, D * b:D * (b + 1)], seqT[:, first:first + KW],
                                   qkv_b_w[:, 2 * D:], start=True, stop=True)
                mm.then_inc(side_ready, 1)

            def proj(row, g, product, walk):
                pe.wait_ge(side_taken, product)
                pe.wait_ge(mix_picked, after(row, TILES, T * g + T))
                pe.matmul(side.rearrange("p (t d) -> p t d", d=D), ones_row[:],
                          bout_row[:].unsqueeze(1).broadcast_to([1, T, D]), start=True, stop=False,
                          skip_group_check=True)
                for t in range(T):
                    mm = pe.matmul(side[:, P * t:P * (t + 1)], mixT[:, T * g + t], out_w[:], start=False,
                                   stop=(t == T - 1), skip_group_check=True)
                mm.then_inc(side_ready, 1)

            steps = {"x_turn": turn_z, "moe_turn": turn_z, "seq_turn": turn_z, "qkv": qkv_step, "attnT": attnT_step,
                     "mlp1": mlp1, "mlp2": mlp2, "route": route, "weighT": weighT, "y_back": y_back, "keys": keys,
                     "queries": queries, "vals": vals_step, "proj": proj}
            Walk(0, True).steps(AHEAD, steps)

            def run(row, walk):
                def gate_up(f, s):
                    n = f * CH + s
                    cols = slice(P * s, P * (s + 1))
                    h, l = z_hi[:, f % 2], z_lo[:, f % 2]
                    for w_hi, w_lo, b, freed, ready in ((gate_hi, gate_lo, 0, silu_ready, gate_ready),
                                                        (up_hi, up_lo, 2, gated_ready, up_ready)):
                        pe.wait_ge(freed, after(row, MOE * CH, n - 1))
                        if f == G and s < 2:
                            pe.wait_ge(probs_ready, after(row, TILES * HG, TILES * HG))
                        dst = bank[b + s % 2]
                        pe.matmul(dst, w_hi[:, cols], h, start=True, stop=False)
                        pe.matmul(dst, w_hi[:, cols], l, start=False, stop=False)
                        pe.matmul(dst, w_lo[:, cols], h, start=False, stop=True).then_inc(ready, 1)

                def spread(f, c):
                    n = f * CH + c
                    if c == 0:
                        pe.wait_ge(side_taken, walk.after_step("weighT", f))
                    if f == G and c < 2:
                        pe.wait_ge(probsT_copied, after(row, TILES * NB, TILES * NB))
                    pe.wait_ge(hid_gated, after(row, MOE * CH, n - 1))
                    pe.matmul(bank[4 + c % 2], expert_sel[:, 2 * c:2 * c + 2].rearrange("p e n -> p (e n)"),
                              combT[:, f % 2], start=True, stop=True).then_inc(spread_ready, 1)

                def down(f, c):
                    pe.wait_ge(hid_gated, after(row, MOE * CH, f * CH + c + 1))
                    if c == 0:
                        pe.wait_ge(y_copied, after(row, MOE, f))
                        if f == G:
                            pe.wait_ge(mix_picked, after(row, TILES, TILES))
                    pe.matmul(bank[6], down_w[:, c], hid[:, c % 2], start=(c == 0),
                              stop=(c == CH - 1)).then_inc(down_done, 1)

                def score(i):
                    if i % T == 0:
                        pe.wait_ge(side_taken, walk.after_step("queries", i // T))
                    if i == 0:
                        pe.wait_ge(silu_ready, after(row, MOE * CH, G * CH))
                        pe.wait_ge(gated_ready, after(row, MOE * CH, G * CH))
                    for hg in range(HG):
                        if i:
                            pe.wait_ge(probs_ready, after(row, TILES * HG, (i - 1) * HG + hg + 1))
                        pe.matmul(bank[hg][:, 0:NB * KW], ident_bf[:],
                                  window[:, min(i, 1)].rearrange("p b k -> p (b k)"), start=True, stop=False,
                                  skip_group_check=True)
                        feats = slice(QB * hg, QB * (hg + 1))
                        for b in range(NB):
                            first = P * i + QB * b
                            mm = pe.matmul(bank[hg][:, KW * b:KW * (b + 1)],
                                           qm[feats, NB * (i % T) + b].rearrange("p j q -> p (j q)"),
                                           keysT[feats, first:first + KW], start=False, stop=(b == NB - 1),
                                           tile_position=(QB * hg, 0), skip_group_check=True)
                        mm.then_inc(scores_ready, 1)

                def mix(i):
                    pe.wait_ge(probs_normed, after(row, TILES, i + 1))
                    if i == 0:
                        pe.wait_ge(hid_gated, after(row, MOE * CH, G * CH))
                        pe.wait_ge(y_copied, after(row, MOE, G))
                    for b in range(NB):
                        pe.wait_ge(probsT_copied, after(row, TILES * NB, i * NB + b - 1))
                        for hg in range(HG):
                            mm = pe.transpose(bank[4 + b % 2][0:KW, P * hg:P * (hg + 1)],
                                              probs[:, i % 2, hg * NB + b], ident[:])
                        mm.then_inc(probsT_ready, 1)
                    pe.wait_ge(side_taken, walk.after_step("vals", i))
                    if i:
                        pe.wait_ge(mix_picked, after(row, TILES, i))
                    for b in range(NB):
                        pe.wait_ge(probsT_copied, after(row, TILES * NB, i * NB + b + 1))
                        for hg in range(HG):
                            feats = slice(QB * hg, QB * (hg + 1))
                            mm = pe.matmul(bank[6][feats, P * b:P * (b + 1)],
                                           vals[:, i % 2, D * b + QB * hg:D * b + QB * (hg + 1)],
                                           probsT[:, b, P * hg:P * (hg + 1)], start=True, stop=True,
                                           tile_position=(0, QB * hg))
                    mm.then_inc(mix_ready, 1)

                for stage in PLAN:
                    kind, f = stage
                    if kind == "moe":
                        for s in range(CH + 2):
                            if s < CH:
                                gate_up(f, s)
                                spread(f, s)
                            if s >= 2:
                                down(f, s - 2)
                            walk.slot(stage, s, steps)
                    else:
                        for i in range(TILES):
                            score(i)
                            if i:
                                mix(i - 1)
                            walk.slot(stage, i, steps)
                        mix(TILES - 1)

            rows_of(pe, run)


_NAMES = ("x", "wqkv_a", "lam", "g1", "g2", "g3", "w1", "w2", "wqkv_b", "wout", "bout", "wgate", "wg", "wu", "wd")


def kernel(L0_attn_a_x, L0_attn_a_Wq, L0_attn_a_Wk, L0_attn_a_Wv, L0_attn_a_lambda_params, L0_attn_a_g1,
           L0_attn_a_g2, L0_attn_a_g3, L0_attn_a_W1, L0_attn_a_W2, L0_attn_b_w_qkv, L0_attn_b_w_out,
           L0_attn_b_b_out, L0_ffn_gate_w, L0_ffn_gate_up_w, L0_ffn_down_w):
    import concourse.bacc as bacc
    from concourse.bass_utils import run_bass_kernel_spmd

    gate_up = np.transpose(np.asarray(L0_ffn_gate_up_w), (2, 0, 1))
    arrays = (
        np.reshape(np.asarray(L0_attn_a_x), (ROWS * SEQ, D)),
        np.transpose(np.concatenate([np.asarray(a) for a in (L0_attn_a_Wq, L0_attn_a_Wk, L0_attn_a_Wv)])),
        L0_attn_a_lambda_params, L0_attn_a_g1, L0_attn_a_g2, L0_attn_a_g3,
        np.transpose(np.asarray(L0_attn_a_W1)), np.transpose(np.asarray(L0_attn_a_W2)),
        np.transpose(np.asarray(L0_attn_b_w_qkv)), np.transpose(np.asarray(L0_attn_b_w_out)), L0_attn_b_b_out,
        np.transpose(np.asarray(L0_ffn_gate_w)),
        np.reshape(gate_up[:, :, 0:ED], (D, NE * ED)), np.reshape(gate_up[:, :, ED:], (D, NE * ED)),
        np.reshape(np.transpose(np.asarray(L0_ffn_down_w), (0, 2, 1)), (NE * ED, D)),
    )
    nc = bacc.Bacc("TRN2", target_bir_lowering=False, num_devices=1)
    feeds, args = {}, []
    for name, a in zip(_NAMES, arrays):
        a = np.ascontiguousarray(a)
        feeds[name] = a
        args.append(nc.dram_tensor(name, a.shape, mybir.dt.from_np(a.dtype), kind="ExternalInput").ap())
    args.append(nc.dram_tensor("out", (ROWS * SEQ, D), F32, kind="ExternalOutput").ap())
    hybrid_block(nc, *args)
    ran = run_bass_kernel_spmd(nc, [feeds], core_ids=[0])
    return np.reshape(ran.results[0]["out"], (ROWS, SEQ, D))
```
